# Optimizing a Trainium2 kernel written in Bass

```python
import numpy as np
import jax
import jax.numpy as jnp

def _softmax(x, axis=-1):
    return jax.nn.softmax(x, axis=axis)

def _gelu(x):
    return jax.nn.gelu(x, approximate=True)

def _silu(x):
    return jax.nn.silu(x)

def _sigmoid(x):
    return jax.nn.sigmoid(x)

def _layernorm(x, axis=-1, eps=1e-05):
    m = jnp.mean(x, axis=axis, keepdims=True)
    v = jnp.var(x, axis=axis, keepdims=True)
    return (x - m) / jnp.sqrt(v + eps)

def _scatter_add(tgt, idx, src, axis=0):
    return tgt.at[idx].add(src)

def _segment_sum(src, seg, n):
    return jax.ops.segment_sum(src, seg, n)
kernel_name = 'mk_gnn_resnorm_d2_gnn_r8_77c99c'

def setup_inputs(seed: int=0):
    np.random.seed(seed)
    _w = jnp.asarray

    def _rec_inputs():
        import jax
        import jax.numpy as jnp
        _gk = jax.random.key(seed)
        x = -0.0003713 + 1 * jax.random.normal(jax.random.fold_in(_gk, 1), (12500, 128), jnp.float32)
        _s = jax.random.randint(jax.random.fold_in(_gk, 2), (200000,), 0, 12500, jnp.int32)
        _d = jax.random.randint(jax.random.fold_in(_gk, 3), (200000,), 0, 12500, jnp.int32)
        _loop = jnp.arange(12500, dtype=jnp.int32)
        src = jnp.concatenate([_s, _d, _loop])
        dst = jnp.concatenate([_d, _s, _loop])
        _o = jnp.argsort(dst, stable=True)
        src = src[_o]
        dst = dst[_o]
        return (x, src, dst)
    x, src, dst = _rec_inputs()

    def _L0_gnn_setup():
        import jax, jax.numpy as jnp
        import numpy as np
        N = 12500
        E = 200000
        IN_CH = 128
        OUT_CH = 128
        key = jax.random.key(seed)
        k1, k2, k3, k4, k5, k6 = jax.random.split(key, 6)
        x = jax.random.normal(k1, (N, IN_CH), dtype=jnp.float32)
        src = jax.random.randint(k2, (E,), 0, N, dtype=jnp.int32)
        dst = jax.random.randint(k3, (E,), 0, N, dtype=jnp.int32)
        bound = 1.0 / np.sqrt(IN_CH)
        W1 = jax.random.uniform(k4, (OUT_CH, IN_CH), minval=-bound, maxval=bound, dtype=jnp.float32)
        b1 = jax.random.uniform(k5, (OUT_CH,), minval=-bound, maxval=bound, dtype=jnp.float32)
        W2 = jax.random.uniform(k6, (OUT_CH, IN_CH), minval=-bound, maxval=bound, dtype=jnp.float32)
        return {'x': x, 'W1': W1, 'b1': b1, 'W2': W2, 'src': src, 'dst': dst}
    _L0_gnn_all = _L0_gnn_setup()
    _L0_gnn_in = {k: v for k, v in _L0_gnn_all.items() if k in ('W1', 'b1', 'W2')}
    del _L0_gnn_all

    def _L1_gnn_setup():
        import jax, jax.numpy as jnp
        import numpy as np
        N_NODES = 6250
        N_EDGES = 100000
        IN_CH = 128
        OUT_CH = 128
        MLP_HID = 64
        key = jax.random.key(seed)
        ks = jax.random.split(key, 8)
        x = jax.random.normal(ks[0], (N_NODES, IN_CH), dtype=jnp.float32)
        edge_index = jax.random.randint(ks[1], (2, N_EDGES), 0, N_NODES, dtype=jnp.int64)
        s1 = 1.0 / np.sqrt(2 * IN_CH)
        mlp_w1 = jax.random.uniform(ks[2], (2 * IN_CH, MLP_HID), jnp.float32, -s1, s1)
        mlp_b1 = jax.random.uniform(ks[3], (MLP_HID,), jnp.float32, -s1, s1)
        s2 = 1.0 / np.sqrt(MLP_HID)
        mlp_w2 = jax.random.uniform(ks[4], (MLP_HID, 1), jnp.float32, -s2, s2)
        mlp_b2 = jax.random.uniform(ks[5], (1,), jnp.float32, -s2, s2)
        s3 = 1.0 / np.sqrt(IN_CH)
        conv_w = jax.random.uniform(ks[6], (IN_CH, OUT_CH), jnp.float32, -s3, s3)
        conv_b = jnp.zeros((OUT_CH,), jnp.float32)
        return {'x': x, 'edge_index': edge_index, 'mlp_w1': mlp_w1, 'mlp_b1': mlp_b1, 'mlp_w2': mlp_w2, 'mlp_b2': mlp_b2, 'conv_w': conv_w, 'conv_b': conv_b}
    _L1_gnn_all = _L1_gnn_setup()
    _L1_gnn_in = {k: v for k, v in _L1_gnn_all.items() if k in ('mlp_w1', 'mlp_b1', 'mlp_w2', 'mlp_b2', 'conv_w', 'conv_b')}
    del _L1_gnn_all
    return {'x': x, 'src': src, 'dst': dst, 'L0_gnn_W1': _L0_gnn_in['W1'], 'L0_gnn_b1': _L0_gnn_in['b1'], 'L0_gnn_W2': _L0_gnn_in['W2'], 'L1_gnn_mlp_w1': _L1_gnn_in['mlp_w1'], 'L1_gnn_mlp_b1': _L1_gnn_in['mlp_b1'], 'L1_gnn_mlp_w2': _L1_gnn_in['mlp_w2'], 'L1_gnn_mlp_b2': _L1_gnn_in['mlp_b2'], 'L1_gnn_conv_w': _L1_gnn_in['conv_w'], 'L1_gnn_conv_b': _L1_gnn_in['conv_b']}

def reference(x, src, dst, L0_gnn_W1, L0_gnn_b1, L0_gnn_W2, L1_gnn_mlp_w1, L1_gnn_mlp_b1, L1_gnn_mlp_w2, L1_gnn_mlp_b2, L1_gnn_conv_w, L1_gnn_conv_b):
    import jax
    import jax.numpy as jnp

    def _L0_gnn_ref(x, W1, b1, W2, src, dst):
        import jax, jax.numpy as jnp
        import numpy as np
        N = 12500
        E = 200000
        IN_CH = 128
        OUT_CH = 128
        n = x.shape[0]
        x1 = x @ W1.T + b1
        x2 = x @ W2.T
        deg = jax.ops.segment_sum(jnp.ones((src.shape[0],), dtype=x.dtype), dst, num_segments=n)[:, None]
        agg = jax.ops.segment_sum(x2[src], dst, num_segments=n)
        return (x1 - x2) * deg + agg

    def _L1_gnn_ref(x, edge_index, mlp_w1, mlp_b1, mlp_w2, mlp_b2, conv_w, conv_b):
        import jax, jax.numpy as jnp
        import numpy as np
        N_NODES = 6250
        N_EDGES = 100000
        IN_CH = 128
        OUT_CH = 128
        MLP_HID = 64
        n = x.shape[0]
        row, col = (edge_index[0], edge_index[1])
        edge_feat = jnp.concatenate([x[row], x[col]], axis=-1)
        h = jax.nn.gelu(edge_feat @ mlp_w1 + mlp_b1, approximate=False)
        edge_weight = jax.nn.sigmoid(h @ mlp_w2 + mlp_b2)[:, 0]
        loop = jnp.arange(n, dtype=row.dtype)
        row_f = jnp.concatenate([row, loop])
        col_f = jnp.concatenate([col, loop])
        ew_f = jnp.concatenate([edge_weight, jnp.ones((n,), x.dtype)])
        deg = jax.ops.segment_sum(ew_f, col_f, num_segments=n)
        dinv = jnp.where(deg > 0, jax.lax.rsqrt(deg), 0.0)
        norm = dinv[row_f] * ew_f * dinv[col_f]
        xt = x @ conv_w
        msg = xt[row_f] * norm[:, None]
        out = jax.ops.segment_sum(msg, col_f, num_segments=n)
        return out + conv_b
    edge_index = jnp.stack([src, dst])
    x = _layernorm(x + _L0_gnn_ref(x, L0_gnn_W1, L0_gnn_b1, L0_gnn_W2, src, dst), axis=-1)
    x = _layernorm(x + _L1_gnn_ref(x, edge_index, L1_gnn_mlp_w1, L1_gnn_mlp_b1, L1_gnn_mlp_w2, L1_gnn_mlp_b2, L1_gnn_conv_w, L1_gnn_conv_b), axis=-1)
    return x

_drawn_inputs = setup_inputs


def setup_inputs(seed=0):
    import zlib

    import numpy as np

    out = dict(_drawn_inputs(seed))
    spreads = {'L1_gnn_conv_b': (0.0, 0.1)}
    factors = {'L1_gnn_mlp_w1': 6.033, 'L1_gnn_mlp_b1': 8.0, 'L1_gnn_mlp_w2': 5.818}
    for name, (base, spread) in spreads.items():
        noise = np.random.default_rng([zlib.crc32(name.encode()), seed]).standard_normal(out[name].shape)
        drawn = base * np.exp(spread * noise) if base else spread * noise
        out[name] = jnp.asarray(drawn.astype(out[name].dtype))
    for name, factor in factors.items():
        out[name] = (out[name] * factor).astype(out[name].dtype)
    return out
```

```python
import concourse.bass as bass
from concourse import mybir
from concourse.alu_op_type import AluOpType as ALU
from contextlib import ExitStack

F32 = mybir.dt.float32
I32 = mybir.dt.int32
ACT = mybir.ActivationFunctionType
AX = mybir.AxisListType.X

P = 128
UNITS = 8
BATCH = P * UNITS
WIN = 64
SLOTS = 4
BT = 7
BLK = BT * P
EPS = 1e-5


def graph_kernel(nc, x, src, dst, W1, b1, W2, mlp_w1, mlp_b1, mlp_w2, mlp_b2, conv_w, conv_b, out):
    N, C = x.shape
    E = src.shape[0]
    H = mlp_w1.shape[1]
    assert C == P and H == WIN
    ROW = H + C
    NBLK = -(-N // BLK)
    NT = NBLK * BT
    NPAD = NT * P
    COLS = NPAD + WIN
    assert NT <= P
    NG = -(-E // (BATCH * SLOTS)) * SLOTS
    NB = NG // SLOTS
    CH = -(-NG // P)
    FULL = E // BATCH
    REST = E - FULL * BATCH
    PAD_DST = 2 * COLS
    WIN_BITS = WIN.bit_length() - 1
    MAX_ROUNDS = NPAD // WIN + 1

    x_pad = nc.dram_tensor("x_pad", (NPAD, C), F32, kind="Internal").ap()
    table1 = nc.dram_tensor("table1", (NPAD, ROW), F32, kind="Internal").ap()
    table2 = nc.dram_tensor("table2", (NPAD, C), F32, kind="Internal").ap()
    dst_part = nc.dram_tensor("dst_part", (COLS, H), F32, kind="Internal").ap()
    deg_lin = nc.dram_tensor("deg_lin", (2, NPAD), F32, kind="Internal").ap()

    ctx = ExitStack()
    with ctx:
        def sb(name, shape, dt=F32):
            return ctx.enter_context(nc.sbuf_tensor(name, shape, dt))

        def sem(name):
            return ctx.enter_context(nc.semaphore(name))

        def sems(name, n):
            return [sem(f"{name}{i}") for i in range(n)]

        acc = sb("acc", [P, COLS])
        y_all = sb("y_all", [P, COLS])
        src_all = sb("src_all", [P, NG * UNITS], I32)
        dst_rel = sb("dst_rel", [P, NG * UNITS])
        ew_all = sb("ew_all", [P, NG * UNITS])
        rows = sb("rows", [P, SLOTS, UNITS, ROW])
        onehot = sb("onehot", [P, SLOTS, UNITS, WIN])
        idx = sb("idx", [P, SLOTS, UNITS], I32)
        win_base = sb("win_base", [1, NG], I32)
        win_cur = sb("win_cur", [1, NG], I32)
        iota_i = sb("iota_i", [P, WIN], I32)
        iota0 = sb("iota0", [P, WIN])
        iota_cur = sb("iota_cur", [P, WIN])
        ident = sb("ident", [P, P])
        ones = sb("ones", [P, P])
        gmin_t = sb("gmin_t", [P, CH])
        span_t = sb("span_t", [P, CH])
        span1 = sb("span1", [P, 1])
        rounds_i = sb("rounds_i", [1, 2], I32)
        w_raw = sb("w_raw", [P, 2, C])
        w_diff = sb("w_diff", [P, C])
        wd_t = sb("wd_t", [P, C])
        w2_t = sb("w2_t", [P, C])
        w_ab = sb("w_ab", [P, 2, H])
        cw = sb("cw", [P, C])
        bias = sb("bias", [P, 3, C])
        w2_row = sb("w2_row", [P, H + 1])
        conv_bias = sb("conv_bias", [P, C])
        minus_half = sb("minus_half", [P, NT])
        zeros = sb("zeros", [P, C])
        w2_all = sb("w2_all", [P, H + 1])
        deg_t = sb("deg_t", [P, P])
        degn = sb("degn", [P, NT])
        scratch = sb("scratch", [P, 5 * BLK])
        bn = sb("bn", [P, BT, 6])
        mv = sb("mv", [P, BT, 2])
        rstd = sb("rstd", [P, BT])

        x_blk = scratch[:, 0:BLK].rearrange("p (t c) -> p t c", c=C)
        agg_blk = scratch[:, BLK:2 * BLK]
        xt_blk = scratch[:, 2 * BLK:3 * BLK]
        v_blk = scratch[:, 3 * BLK:4 * BLK].rearrange("p (t c) -> p t c", c=C)
        y_blk = scratch[:, 4 * BLK:5 * BLK].rearrange("p (t c) -> p t c", c=C)
        rows_flat = rows[:, :, :, :].rearrange("p s u c -> p (s u c)")
        t1_blk = rows_flat[:, 0:BT * ROW].rearrange("p (t c) -> p t c", c=ROW)
        d_blk = rows_flat[:, BT * ROW:BT * (ROW + H)].rearrange("p (t c) -> p t c", c=H)
        z_edge = scratch[:, 0:SLOTS * UNITS * H].rearrange("p (s u h) -> p s u h", s=SLOTS, u=UNITS)
        o1 = SLOTS * UNITS * H
        oh_t = scratch[0:WIN, o1:o1 + 2 * BATCH].rearrange("w (b u p) -> w b u p", b=2, u=UNITS)
        gelu_edge = sb("gelu_edge", [P, 2, UNITS, H])
        d_win = sb("d_win", [WIN, SLOTS, H])
        logit = sb("logit", [P, SLOTS, UNITS])
        tanh_edge = sb("tanh_edge", [P, SLOTS, UNITS])
        mask = sb("mask", [P, SLOTS, UNITS])
        ew = sb("ew", [P, SLOTS, UNITS])
        assert o1 + 2 * BATCH <= 5 * BLK

        raw_dst = y_all[:, 0:CH * BATCH].bitcast(I32).rearrange("g (c e) -> g c e", c=CH)
        raw_src = y_all[:, CH * BATCH:2 * CH * BATCH].bitcast(I32).rearrange("g (c e) -> g c e", c=CH)
        raw_f = acc[:, 0:CH * BATCH].rearrange("g (c e) -> g c e", c=CH)
        gmin = acc[:, CH * BATCH:CH * BATCH + NG]
        gmax = acc[:, CH * BATCH + NG:CH * BATCH + 2 * NG]
        capped = acc[:, CH * BATCH + 2 * NG:CH * BATCH + 2 * NG + NG * UNITS]
        base_f = y_all[:, 0:NG]
        assert CH * BATCH + 2 * NG + NG * UNITS <= COLS
        deg0_row = y_all[0:1, :]
        deg1_row = acc[0:1, :]

        psum = ctx.enter_context(nc.psum_tensor("psum", [P, 8, 512], F32))
        ps_flat = psum[:, :, :].rearrange("p b n -> p (b n)")

        s_w = sem("s_weights_loaded")
        s_dst = sem("s_dst_loaded")
        s_src = sem("s_src_loaded")
        s_xpad = sem("s_x_padded")
        s_iota = sem("s_iota")
        s_cst = sem("s_constants")
        s_pads = sem("s_pads_set")
        s_float = sem("s_indices_as_float")
        s_tr = sem("s_chunk_transposed")
        s_ev = sem("s_chunk_evacuated")
        s_pp = sem("s_prologue_product")
        s_pv = sem("s_prologue_vector")
        s_win = sem("s_windows_ready")
        s_zero = sem("s_zero_rows")
        s_gate = sem("s_gate")
        s_var = sem("s_variances_ready")
        s_rstd = sem("s_powers_ready")
        s_chain = sem("s_prologue_chain")
        CHAIN0, CHAIN2 = 6, 5

        class Pass:

            def __init__(self, name):
                self.idx_full = sems(f"{name}_idx_full", SLOTS)
                self.rows_full = sems(f"{name}_rows_full", SLOTS)
                self.onehot = sem(f"{name}_onehot_ready")
                self.used = sem(f"{name}_slot_used")
                self.added = sem(f"{name}_sums_added")
                self.chain = sem(f"{name}_vector_chain")
                self.done = sem(f"{name}_done")

        p0, p1, p2 = Pass("p0"), Pass("p1"), Pass("p2")
        s_dwin = sems("p1_dst_window_full", SLOTS)
        s_oht = sem("p1_onehot_transposed")
        s_ohc = sem("p1_transpose_copied")
        s_z = sem("p1_dst_product")
        s_zc = sem("p1_z_ready")
        s_gelu = sem("p1_gelu_ready")
        s_log = sem("p1_logit_ready")
        s_tanh = sem("p1_tanh_ready")
        s_ew = sem("p1_ew_ready")

        s_dg = sem("s_degree_row_stored")
        s_dgl = sem("s_degree_loaded")
        s_dgt = sem("s_degree_transposed")
        s_dgn = sem("s_degree_ready")
        s_xb = sem("n0_x_block")
        s_ag = sem("n0_sums_copied")
        s_xt = sem("n0_x_transposed")
        s_xc = sem("n0_x_copied")
        s_uv = sem("n0_products")
        s_v0 = sem("n0_vector_chain")
        s_y0 = sem("n0_y_ready")
        s_yt = sem("n0_y_transposed")
        s_yc = sem("n0_y_copied")
        s_ab = sem("n0_table_product")
        s_t1 = sem("n0_table_rows_ready")
        s_ts = sem("n0_table_stored")
        s_s2 = sem("n1_scaled_ready")
        s_s2t = sem("n1_scaled_transposed")
        s_s2c = sem("n1_scaled_copied")
        s_t2 = sem("n1_table_stored")
        s_g2 = sem("n2_sums_copied")
        s_c2 = sem("n2_products")
        s_v2 = sem("n2_vector_chain")
        s_zd = sem("n2_z_ready")
        s_out = sem("s_out_stored")

        block = ctx.enter_context(nc.Block())

        def load_rounds(eng):
            return eng.snap(eng.value_load(rounds_i[0:1, 0:1], min_val=1, max_val=MAX_ROUNDS) * NB)

        def sum_psum(s):
            return psum[:, s, 0:WIN], psum[0:1, s, WIN:2 * WIN]

        def agg_blk2(b):
            return scratch[:, (b % 2) * BLK:(b % 2 + 1) * BLK]

        def degrees(sp, p, row, n):
            sp.wait_ge(p.done, 1)
            sp.dma_start(deg_lin[n:n + 1, :], row[:, 0:NPAD]).then_inc(s_dg, 16)
            sp.wait_ge(s_dg, 16 * (n + 1))
            sp.dma_start(deg_t[0:NT, :], deg_lin[n, :].rearrange("(t p) -> t p", p=P)).then_inc(s_dgl, 16)

        @block.sync
        def _(sp):
            sp.wait_ge(s_pads, 1)
            for raw, ind, done in ((raw_dst, dst, s_dst), (raw_src, src, s_src)):
                for c in range(CH):
                    lo, hi = c * P, min(FULL, (c + 1) * P)
                    if hi > lo:
                        sp.dma_start(raw[0:hi - lo, c, :],
                                     ind[lo * BATCH:hi * BATCH].rearrange("(g e) -> g e", e=BATCH)).then_inc(done, 16)
                if REST:
                    sp.dma_start(raw[FULL % P:FULL % P + 1, FULL // P, 0:REST],
                                 ind[FULL * BATCH:E].rearrange("(g e) -> g e", g=1)).then_inc(done, 16)
            for t, w in enumerate((W1, W2)):
                sp.dma_start(w_raw[:, t, :], w).then_inc(s_w, 16)
            sp.dma_start(w_ab[:, 0, :], mlp_w1[0:C, :]).then_inc(s_w, 16)
            sp.dma_start(w_ab[:, 1, :], mlp_w1[C:2 * C, :]).then_inc(s_w, 16)
            sp.dma_start(cw[:, :], conv_w).then_inc(s_w, 16)
            sp.wait_ge(s_cst, 1)
            sp.dma_start(bias[0:1, 0, :], b1.rearrange("(a n) -> a n", a=1)).then_inc(s_w, 16)
            sp.dma_start(bias[0:1, 1, H:2 * H], mlp_b1.rearrange("(a n) -> a n", a=1)).then_inc(s_w, 16)
            sp.dma_start(bias[0:1, 2, :], conv_b.rearrange("(a n) -> a n", a=1)).then_inc(s_w, 16)
            sp.dma_start(w2_row[0:1, 0:H], mlp_w2.rearrange("h a -> a h")).then_inc(s_w, 16)
            sp.dma_start(w2_row[0:1, H:H + 1], mlp_b2.rearrange("(a n) -> a n", a=1)).then_inc(s_w, 16)
            sp.dma_start(x_pad[0:N, :], x).then_inc(s_xpad, 16)
            for lo in range(N, NPAD, P):
                m = min(P, NPAD - lo)
                sp.dma_start(x_pad[lo:lo + m, :], zeros[0:m, :]).then_inc(s_xpad, 16)
            sp.dma_start(dst_part[NPAD:COLS, :], zeros[0:WIN, 0:H]).then_inc(s_zero, 16)
            sp.wait_ge(s_win, 1)
            end = load_rounds(sp)

            def load_idx(p, c, b, s):
                sp.wait_ge(p.used, c * SLOTS + (s + 1))
                at = b * (SLOTS * UNITS) + s * UNITS
                sp.dma_start(idx[:, s, :], src_all[:, bass.ds(at, UNITS)]).then_inc(p.idx_full[s], 16)

            with sp.Fori(0, end, NB) as c0:
                with sp.Fori(0, NB) as b:
                    c = c0 + b
                    for s in range(SLOTS):
                        load_idx(p0, c, b, s)
            degrees(sp, p0, deg0_row, 0)
            sp.wait_ge(s_xpad, 16 * (1 + -(-(NPAD - N) // P)))
            for b in range(NBLK):
                if b >= 1:
                    sp.wait_ge(s_v0, CHAIN0 * b)
                sp.dma_start(x_blk, x_pad[b * BLK:(b + 1) * BLK, :].rearrange("(t p) c -> p t c", p=P)).then_inc(s_xb, 16)
                sp.wait_ge(s_t1, b + 1)
                sp.dma_start(table1[b * BLK:(b + 1) * BLK, :].rearrange("(t p) c -> p t c", p=P), t1_blk).then_inc(s_ts, 16)
                sp.dma_start(dst_part[b * BLK:(b + 1) * BLK, :].rearrange("(t p) c -> p t c", p=P), d_blk).then_inc(s_ts, 16)
            sp.wait_ge(s_ts, 32 * NBLK)
            sp.wait_ge(s_zero, 16)
            with sp.Fori(0, end, NB) as c0:
                sp.wait_ge(s_win, end + c0 + 1)
                sp.sem_inc(s_gate)
                with sp.Fori(0, NB) as b:
                    c = c0 + b
                    for s in range(SLOTS):
                        load_idx(p1, c, b, s)
                        w = sp.value_load(win_cur[0:1, bass.ds(b * SLOTS + s, 1)], min_val=0, max_val=NPAD)
                        sp.dma_start(d_win[:, s, :], dst_part[bass.ds(w, WIN), :]).then_inc(s_dwin[s], 16)
            degrees(sp, p1, deg1_row, 1)
            for b in range(NBLK):
                sp.wait_ge(s_s2, b + 1)
                sp.dma_start(table2[b * BLK:(b + 1) * BLK, :].rearrange("(t p) c -> p t c", p=P), v_blk).then_inc(s_t2, 16)
            with sp.Fori(0, end, NB) as c0:
                with sp.Fori(0, NB) as b:
                    c = c0 + b
                    for s in range(SLOTS):
                        load_idx(p2, c, b, s)
            stores = 0
            for b in range(NBLK):
                sp.wait_ge(s_zd, b + 1)
                tiles = min(BT, max(0, (N - b * BLK) // P))
                lo = b * BLK
                if tiles:
                    sp.dma_start(out[lo:lo + tiles * P, :].rearrange("(t p) c -> p t c", p=P),
                                 y_all[:, lo:lo + tiles * P].rearrange("p (t c) -> p t c", c=C)).then_inc(s_out, 16)
                    stores += 1
                left = min(N - lo - tiles * P, P) if tiles < BT else 0
                if left > 0:
                    sp.dma_start(out[lo + tiles * P:lo + tiles * P + left, :],
                                 y_all[0:left, lo + tiles * P:lo + (tiles + 1) * P]).then_inc(s_out, 16)
                    stores += 1
            sp.wait_ge(s_out, 16 * stores)

        @block.gpsimd
        def _(pool):
            pool.iota(iota_i[:, :], pattern=[[1, WIN]], base=0, channel_multiplier=0).then_inc(s_iota, 1)
            pool.memset(ident[:, :], 0.0).then_inc(s_iota, 1)
            pool.wait_ge(s_iota, 2)
            pool.affine_select(out=ident[:, :], in_=ident[:, :], compare_op=ALU.not_equal, fill=1.0, base=0,
                               pattern=[[-1, P]], channel_multiplier=1).then_inc(s_iota, 1)
            pool.wait_ge(s_win, 1)
            end = load_rounds(pool)

            def gather(p, table, width):
                with pool.Fori(0, end) as c:
                    for s in range(SLOTS):
                        pool.wait_ge(p.idx_full[s], (c + 1) * 16)
                        pool.sem_inc(s_gate)
                        for u in range(UNITS):
                            pool.indirect_dma_start(
                                out=rows[:, s, u, 0:width], out_offset=None, in_=table,
                                in_offset=bass.IndirectOffsetOnAxis(idx[:, s, u:u + 1], 0)).then_inc(p.rows_full[s], 16)

            gather(p0, x, C)

            def inverse_deviations(made):
                for b in range(NBLK):
                    pool.wait_ge(s_var, made + b + 1)
                    nc.gpsimd.tensor_tensor(rstd[:, :], rstd[:, :], minus_half[:, 0:BT], ALU.pow).then_inc(s_rstd, 1)

            inverse_deviations(0)
            pool.wait_ge(s_ts, 32 * NBLK)
            gather(p1, table1, ROW)
            pool.wait_ge(s_dgn, 2)
            nc.gpsimd.tensor_tensor(degn[:, :], degn[:, :], minus_half[:, :], ALU.pow).then_inc(s_rstd, 1)
            pool.wait_ge(s_t2, 16 * NBLK)
            gather(p2, table2, C)
            inverse_deviations(NBLK)

        @block.tensor
        def _(pe):
            pe.wait_ge(s_iota, 3)
            pe.wait_ge(s_cst, 1)
            n = 0
            for a in range(2):
                for c in range(CH):
                    pe.wait_ge(s_float, a * CH + c + 1)
                    for h in range(UNITS // 4):
                        if n >= 4:
                            pe.wait_ge(s_ev, n - 3)
                        for u in range(4):
                            q = 4 * h + u
                            last = nc.tensor.transpose(psum[:, n % 4, u * P:(u + 1) * P],
                                                       raw_f[:, c, q * P:(q + 1) * P], ident[:, :])
                        last.then_inc(s_tr, 1)
                        n += 1
            pe.wait_ge(s_pv, 1)
            for c in range(CH):
                m = min(P, NG - c * P)
                nc.tensor.transpose(psum[0:m, 4, c * P:(c + 1) * P], gmin[:, c * P:c * P + m], ident[:, :])
                last = nc.tensor.transpose(psum[0:m, 5, c * P:(c + 1) * P], gmax[:, c * P:c * P + m], ident[:, :])
            last.then_inc(s_pp, 1)
            pe.wait_ge(s_pv, 2)
            for c in range(CH):
                m = min(P, NG - c * P)
                nc.tensor.matmul(psum[:, 6, c * P:c * P + m], ones[0:m, :], raw_f[0:m, 0, c * P:c * P + m],
                                 start=True, stop=True)
            nc.tensor.transpose(psum[0:1, 7, 0:P], span1[:, :], ident[:, :]).then_inc(s_pp, 1)
            pe.wait_ge(s_pv, 3)
            nc.tensor.transpose(psum[:, 0, 0:P], w_diff[:, :], ident[:, :])
            nc.tensor.transpose(psum[:, 0, P:2 * P], w_raw[:, 1, :], ident[:, :])
            nc.tensor.matmul(psum[:, 0, 2 * P:2 * P + H + 1], ones[:, :], w2_row[:, :], start=True, stop=True)
            nc.tensor.matmul(psum[:, 1, 0:C], ones[:, :], bias[:, 2, :], start=True, stop=True).then_inc(s_pp, 1)

            def load_end():
                pe.wait_ge(s_win, 1)
                return load_rounds(pe)

            end = load_end()
            pe.sem_inc(p0.used, SLOTS)

            def sums(p, c, s, deg):
                pe.wait_ge(p.rows_full[s], (c + 1) * (16 * UNITS))
                pe.wait_ge(p.onehot, c * SLOTS + (s + 1))
                pe.wait_ge(p.added, c * SLOTS + (s + 1))
                total, count = sum_psum(s)
                for u in range(UNITS):
                    last = nc.tensor.matmul(total, rows[:, s, u, 0:C], onehot[:, s, u, :],
                                            start=(u == 0), stop=(u == UNITS - 1))
                if deg:
                    for u in range(UNITS):
                        last = nc.tensor.matmul(count, ones[:, 0:1], onehot[:, s, u, :],
                                                start=(u == 0), stop=(u == UNITS - 1))
                last.then_inc(p.used, 1)

            with pe.Fori(0, end) as c:
                for s in range(SLOTS):
                    sums(p0, c, s, True)

            def degree_tile(n):
                pe.wait_ge(s_dgl, 16 * (n + 1))
                nc.tensor.transpose(psum[:, 7, 0:NT], deg_t[0:NT, :], ident[0:NT, 0:NT]).then_inc(s_dgt, 1)

            degree_tile(0)
            for b in range(NBLK):
                pe.wait_ge(s_xb, 16 * (b + 1))
                if b:
                    pe.wait_ge(s_t1, b)
                for t in range(BT):
                    last = nc.tensor.transpose(ps_flat[:, t * P:(t + 1) * P], x_blk[:, t, :], ident[:, :])
                last.then_inc(s_xt, 1)
                pe.wait_ge(s_xc, b + 1)
                pe.wait_ge(s_ag, b + 1)
                for t in range(BT):
                    u_out = ps_flat[:, 1024 + t * P:1024 + (t + 1) * P]
                    nc.tensor.matmul(u_out, xt_blk[:, t * P:(t + 1) * P], wd_t[:, :], start=True, stop=False)
                    nc.tensor.matmul(u_out, ones[:, :], bias[:, 0, :], start=False, stop=True)
                for t in range(BT):
                    last = nc.tensor.matmul(ps_flat[:, 2048 + t * P:2048 + (t + 1) * P],
                                            agg_blk[:, t * P:(t + 1) * P], w2_t[:, :], start=True, stop=True)
                last.then_inc(s_uv, 1)
                pe.wait_ge(s_y0, b + 1)
                for t in range(BT):
                    last = nc.tensor.transpose(ps_flat[:, t * P:(t + 1) * P], y_blk[:, t, :], ident[:, :])
                last.then_inc(s_yt, 1)
                pe.wait_ge(s_yc, b + 1)
                for t in range(BT):
                    ab = ps_flat[:, 1024 + t * P:1024 + (t + 1) * P]
                    nc.tensor.matmul(ab, xt_blk[:, t * P:(t + 1) * P], w_ab[:, :, :].rearrange("p a h -> p (a h)"),
                                     start=True, stop=False)
                    last = nc.tensor.matmul(ab, ones[:, :], bias[:, 1, :], start=False, stop=True)
                last.then_inc(s_ab, 1)
            pe.sem_inc(p1.used, SLOTS)

            def oh_psum(b):
                return ps_flat[0:WIN, b * 1024:(b + 1) * 1024]

            def turn(c, s):
                pe.wait_ge(p1.onehot, c * SLOTS + (s + 1))
                pe.wait_ge(s_ohc, c * SLOTS + (s + 1))
                pe.sem_inc(s_gate)
                for u in range(UNITS):
                    last = nc.tensor.transpose(oh_psum(s % 2)[:, u * P:(u + 1) * P], onehot[:, s, u, :], ident[:, :])
                last.then_inc(s_oht, 1)

            def dst_rows(c, s):
                pe.wait_ge(s_dwin[s], (c + 1) * 16)
                pe.wait_ge(s_ohc, c * SLOTS + (s + 3))
                pe.wait_ge(s_zc, c * SLOTS + (s + 1))
                for u in range(UNITS):
                    last = nc.tensor.matmul(psum[:, 4 + s % 2, u * H:(u + 1) * H], oh_t[:, s % 2, u, :],
                                            d_win[:, s, :], start=True, stop=True)
                last.then_inc(s_z, 1)

            def degree_sum(c, s):
                pe.wait_ge(s_ew, c * SLOTS + (s + 1))
                pe.wait_ge(p1.added, c * SLOTS + (s + 1))
                for u in range(UNITS):
                    last = nc.tensor.matmul(psum[0:1, 6 + s % 2, 0:WIN], ew[:, s, u:u + 1], onehot[:, s, u, :],
                                            start=(u == 0), stop=(u == UNITS - 1))
                last.then_inc(p1.used, 1)

            with pe.Fori(0, end) as c:
                turn(c, 0)
                turn(c, 1)
                dst_rows(c, 0)
                turn(c, 2)
                dst_rows(c, 1)
                turn(c, 3)
                for s in range(SLOTS):
                    if s + 2 < SLOTS:
                        dst_rows(c, s + 2)
                    degree_sum(c, s)

            degree_tile(1)
            for b in range(NBLK):
                pe.wait_ge(s_s2, b + 1)
                if b:
                    pe.wait_ge(s_s2c, b)
                for t in range(BT):
                    last = nc.tensor.transpose(ps_flat[:, t * P:(t + 1) * P], v_blk[:, t, :], ident[:, :])
                last.then_inc(s_s2t, 1)
            pe.sem_inc(p2.used, SLOTS)
            pe.wait_ge(s_s2c, NBLK)
            with pe.Fori(0, end) as c:
                for s in range(SLOTS):
                    sums(p2, c, s, False)
            for b in range(NBLK):
                pe.wait_ge(s_g2, b + 1)
                if b >= 2:
                    pe.wait_ge(s_v2, CHAIN2 * (b - 2) + 1)
                for t in range(BT):
                    o = (b % 2) * 1024 + t * P
                    last = nc.tensor.matmul(ps_flat[:, o:o + P], agg_blk2(b)[:, t * P:(t + 1) * P], cw[:, :],
                                            start=True, stop=True)
                last.then_inc(s_c2, 1)

        @block.scalar
        def _(act):
            act.wait_ge(s_win, 1)
            end = load_rounds(act)
            act.wait_ge(p0.done, 1)
            for b in range(NBLK):
                if b:
                    act.wait_ge(s_uv, b)
                nc.scalar.activation(agg_blk, acc[:, b * BLK:(b + 1) * BLK], ACT.Copy).then_inc(s_ag, 1)
                act.wait_ge(s_xt, b + 1)
                if b:
                    act.wait_ge(s_ab, b)
                nc.scalar.activation(xt_blk, ps_flat[:, 0:BLK], ACT.Copy).then_inc(s_xc, 1)
                act.wait_ge(s_yt, b + 1)
                nc.scalar.activation(xt_blk, ps_flat[:, 0:BLK], ACT.Copy).then_inc(s_yc, 1)
                act.wait_ge(s_ab, b + 1)
                if b:
                    act.wait_ge(s_ts, 32 * b)
                ab = ps_flat[:, 1024:1024 + BLK].rearrange("p (t c) -> p t c", c=C)
                nc.scalar.activation(t1_blk[:, :, 0:H], ab[:, :, 0:H], ACT.Copy)
                nc.scalar.activation(d_blk, ab[:, :, H:2 * H], ACT.Copy)
                nc.scalar.activation(t1_blk[:, :, H:ROW], y_blk, ACT.Copy).then_inc(s_t1, 1)

            act.sem_inc(s_ohc, 2)
            with act.Fori(0, end) as c:
                def copy_turned(s):
                    act.wait_ge(s_oht, c * SLOTS + (s + 1))
                    act.wait_ge(s_zc, c * SLOTS + (s + 1))
                    nc.scalar.activation(oh_t[:, s % 2, :, :].rearrange("w u p -> w (u p)"),
                                         ps_flat[0:WIN, (s % 2) * 1024:(s % 2 + 1) * 1024], ACT.Copy).then_inc(s_ohc, 1)

                def weigh(s):
                    act.wait_ge(s_zc, c * SLOTS + (s + 3))
                    nc.scalar.activation(gelu_edge[:, s % 2, :, :], z_edge[:, s, :, :], ACT.Gelu)\
                        .then_inc(s_gelu, 1)
                    act.wait_ge(s_log, c * SLOTS + (s + 1))
                    nc.scalar.activation(tanh_edge[:, s, :], logit[:, s, :], ACT.Tanh, scale=0.5,
                                         bias=w2_all[:, H:H + 1]).then_inc(s_tanh, 1)

                copy_turned(0)
                copy_turned(1)
                for s in range(SLOTS):
                    if s + 2 < SLOTS:
                        copy_turned(s + 2)
                    weigh(s)
            for b in range(NBLK):
                act.wait_ge(s_s2t, b + 1)
                nc.scalar.activation(acc[:, b * BLK:(b + 1) * BLK], ps_flat[:, 0:BLK], ACT.Copy).then_inc(s_s2c, 1)
            act.wait_ge(p2.done, 1)
            for b in range(NBLK):
                if b >= 2:
                    act.wait_ge(s_c2, b - 1)
                nc.scalar.activation(agg_blk2(b), acc[:, b * BLK:(b + 1) * BLK], ACT.Copy).then_inc(s_g2, 1)

        @block.vector
        def _(dve):
            made = [0]

            def chain(ins, s=s_chain):
                made[0] += 1
                ins.then_inc(s, 1)
                dve.wait_ge(s, made[0])

            for c in range(FULL // P, CH):
                nc.vector.memset(raw_src[:, c, :], 0)
                nc.vector.memset(raw_dst[:, c, :], PAD_DST)
            nc.vector.memset(zeros[:, :], 0.0).then_inc(s_pads, 1)
            nc.vector.memset(ones[:, :], 1.0)
            nc.vector.memset(span_t[:, :], 0.0)
            nc.vector.memset(minus_half[:, :], -0.5)
            nc.vector.memset(ew_all[:, :], 0.0)
            nc.vector.memset(w2_row[:, :], 0.0)
            nc.vector.memset(bias[:, :, :], 0.0).then_inc(s_cst, 1)
            loads = sum(1 for c in range(CH) if min(FULL, (c + 1) * P) > c * P) + (REST > 0)
            n = 0
            for a, (raw, done, to) in enumerate(((raw_dst, s_dst, dst_rel), (raw_src, s_src, src_all))):
                dve.wait_ge(done, 16 * loads)
                if a:
                    dve.wait_ge(s_tr, n)
                for c in range(CH):
                    nc.vector.tensor_copy(raw_f[:, c, :], raw[:, c, :]).then_inc(s_float, 1)
                for c in range(CH):
                    m = min(P, NG - c * P)
                    for h in range(UNITS // 4):
                        dve.wait_ge(s_tr, n + 1)
                        nc.vector.tensor_copy(
                            to[:, :].rearrange("p (g u) -> p u g", u=UNITS)[:, 4 * h:4 * h + 4, c * P:c * P + m],
                            psum[:, n % 4, :].rearrange("p (u g) -> p u g", u=4)[:, :, 0:m]).then_inc(s_ev, 1)
                        n += 1
                if a == 0:
                    dve.wait_ge(s_ev, n)
                    chain(nc.vector.tensor_scalar(capped, dst_rel[:, :], float(N - 1), None, ALU.min))
                    nc.vector.tensor_reduce(gmin, dst_rel[:, :].rearrange("p (g u) -> p g u", u=UNITS), AX, ALU.min)
                    nc.vector.tensor_reduce(gmax, capped.rearrange("p (g u) -> p g u", u=UNITS), AX, ALU.max)\
                        .then_inc(s_pv, 1)
            dve.wait_ge(s_pp, 1)
            for c in range(CH):
                m = min(P, NG - c * P)
                nc.vector.tensor_reduce(gmin_t[0:m, c:c + 1], psum[0:m, 4, c * P:(c + 1) * P], AX, ALU.min)
                chain(nc.vector.tensor_reduce(span_t[0:m, c:c + 1], psum[0:m, 5, c * P:(c + 1) * P], AX, ALU.max))
                nc.vector.tensor_tensor(span_t[0:m, c:c + 1], span_t[0:m, c:c + 1], gmin_t[0:m, c:c + 1], ALU.subtract)
                chain(nc.vector.tensor_scalar(raw_f[0:m, 0, c * P:c * P + m], ident[0:m, 0:m],
                                              gmin_t[0:m, c:c + 1], None, ALU.mult))
            nc.vector.tensor_reduce(span1[:, :], span_t[:, :], AX, ALU.max).then_inc(s_pv, 1)
            dve.wait_ge(s_pp, 2)
            chain(nc.vector.tensor_scalar(base_f, psum[:, 6, 0:NG], float(NPAD), None, ALU.min))
            nc.vector.tensor_copy(win_base[0:1, :], base_f[0:1, :])
            nc.vector.tensor_copy(win_cur[0:1, :], base_f[0:1, :])
            chain(nc.vector.tensor_tensor(dst_rel[:, :].rearrange("p (g u) -> p g u", u=UNITS),
                                          dst_rel[:, :].rearrange("p (g u) -> p g u", u=UNITS),
                                          base_f.unsqueeze(2).to_broadcast([P, NG, UNITS]), ALU.subtract))
            chain(nc.vector.tensor_reduce(span1[0:1, :], psum[0:1, 7, 0:P], AX, ALU.max))
            chain(nc.vector.tensor_scalar(span1[0:1, :], span1[0:1, :], float(WIN), None, ALU.add))
            chain(nc.vector.tensor_copy(rounds_i[0:1, 1:2], span1[0:1, :]))
            chain(nc.vector.tensor_scalar(rounds_i[0:1, 0:1], rounds_i[0:1, 1:2], WIN_BITS, None,
                                          ALU.logical_shift_right))
            dve.wait_ge(s_iota, 1)
            nc.vector.tensor_copy(iota0[:, :], iota_i[:, :])
            nc.vector.tensor_copy(iota_cur[:, :], iota_i[:, :])
            nc.vector.memset(acc[:, :], 0.0)
            nc.vector.memset(deg0_row, 0.0).then_inc(s_win, 1)
            dve.wait_ge(s_win, 1)
            dve.wait_ge(s_w, 160)
            nc.vector.tensor_tensor(w_diff[:, :], w_raw[:, 0, :], w_raw[:, 1, :], ALU.subtract).then_inc(s_pv, 1)
            dve.wait_ge(s_pp, 3)
            nc.vector.tensor_copy(wd_t[:, :], psum[:, 0, 0:P])
            nc.vector.tensor_copy(w2_t[:, :], psum[:, 0, P:2 * P])
            nc.vector.tensor_scalar(w2_all[:, H:H + 1], psum[:, 0, 2 * P + H:2 * P + H + 1], 0.5, None, ALU.mult)
            nc.vector.tensor_copy(conv_bias[:, :], psum[:, 1, 0:C])
            nc.vector.tensor_copy(w2_all[:, 0:H], psum[:, 0, 2 * P:2 * P + H]).then_inc(p0.added, SLOTS)

            end = load_rounds(dve)

            def dst_cols(b, s):
                return bass.ds(b * (SLOTS * UNITS) + s * UNITS, UNITS)

            def window(b, s):
                return dve.value_load(win_cur[0:1, bass.ds(b * SLOTS + s, 1)], min_val=0, max_val=NPAD)

            def make_onehot(b, s):
                return nc.vector.tensor_tensor(
                    onehot[:, s, :, :],
                    dst_rel[:, dst_cols(b, s)].unsqueeze(2).to_broadcast([P, UNITS, WIN]),
                    iota_cur[:, :].unsqueeze(1).to_broadcast([P, UNITS, WIN]), ALU.is_equal)

            def next_round():
                nc.vector.tensor_scalar(iota_cur[:, :], iota_cur[:, :], float(WIN), None, ALU.add)
                nc.vector.tensor_scalar(win_cur[:, :], win_cur[:, :], float(WIN), float(NPAD), ALU.add, ALU.min)\
                    .then_inc(s_win, NB)

            def end_pass(p, n):
                dve.wait_ge(s_win, end * (n + 1) + 1)
                nc.vector.tensor_copy(iota_cur[:, :], iota0[:, :])
                nc.vector.tensor_copy(win_cur[:, :], win_base[:, :]).then_inc(p.done, 1)
                dve.wait_ge(p.done, 1)

            def sum_pass(p, n, deg):
                with dve.Fori(0, end, NB) as c0:
                    dve.wait_ge(s_win, end * n + c0 + 1)
                    dve.sem_inc(s_gate)
                    with dve.Fori(0, NB) as b:
                        c = c0 + b
                        for s in range(SLOTS):
                            if deg:
                                make_onehot(b, s).then_inc(p.onehot, 1)
                            else:
                                make_onehot(b, s).then_inc(p.chain, 1)
                        if not deg:
                            for s in range(SLOTS):
                                dve.wait_ge(p.chain, c * SLOTS + (s + 1))
                                nc.vector.tensor_tensor(
                                    onehot[:, s, :, :], onehot[:, s, :, :],
                                    ew_all[:, dst_cols(b, s)].unsqueeze(2).to_broadcast([P, UNITS, WIN]),
                                    ALU.mult).then_inc(p.onehot, 1)
                        for s in range(SLOTS):
                            w = window(b, s)
                            dve.wait_ge(p.used, c * SLOTS + (s + 1 + SLOTS))
                            dve.wait_ge(p.added, c * SLOTS + (s + SLOTS))
                            total, count = sum_psum(s)
                            last = nc.vector.tensor_tensor(acc[:, bass.ds(w, WIN)], acc[:, bass.ds(w, WIN)], total,
                                                           ALU.add)
                            if deg:
                                last = nc.vector.tensor_tensor(deg0_row[:, bass.ds(w, WIN)],
                                                               deg0_row[:, bass.ds(w, WIN)], count, ALU.add)
                            last.then_inc(p.added, 1)
                    next_round()
                end_pass(p, n)

            sum_pass(p0, 0, True)

            def degree_tile(n):
                dve.wait_ge(s_dgt, n + 1)
                return nc.vector.tensor_copy(degn[:, :], psum[:, 7, 0:NT])

            degree_tile(0).then_inc(s_dgn, 1)
            dve.wait_ge(s_dgn, 1)

            def layer_norm(link, made):
                for t in range(BT):
                    last = nc.vector.bn_stats(bn[:, t, :], v_blk[:, t, :])
                link(last)
                for t in range(BT):
                    last = nc.vector.bn_aggr(mv[:, t, :], bn[:, t, :])
                link(last)
                nc.vector.tensor_scalar(rstd[:, :], mv[:, :, 1:2].rearrange("p t a -> p (t a)"), EPS, None,
                                        ALU.add).then_inc(s_var, 1)
                dve.wait_ge(s_rstd, made)

            n0 = [0]

            def link0(ins):
                n0[0] += 1
                ins.then_inc(s_v0, 1)
                dve.wait_ge(s_v0, n0[0])

            for b in range(NBLK):
                dve.wait_ge(s_uv, b + 1)
                if b:
                    dve.wait_ge(s_t1, b)
                u_ps = ps_flat[:, 1024:1024 + BLK].rearrange("p (t c) -> p t c", c=C)
                v_ps = ps_flat[:, 2048:2048 + BLK].rearrange("p (t c) -> p t c", c=C)
                link0(nc.vector.tensor_tensor(v_blk, u_ps, degn[:, b * BT:(b + 1) * BT].unsqueeze(2)
                                              .to_broadcast([P, BT, C]), ALU.mult))
                link0(nc.vector.tensor_tensor(v_blk, v_blk, v_ps, ALU.add))
                link0(nc.vector.tensor_tensor(v_blk, v_blk, x_blk, ALU.add))
                layer_norm(link0, b + 1)
                for t in range(BT):
                    last = nc.vector.tensor_scalar(y_blk[:, t, :], v_blk[:, t, :], mv[:, t, 0:1], rstd[:, t:t + 1],
                                                   ALU.subtract, ALU.mult)
                last.then_inc(s_y0, 1)
                dve.wait_ge(s_y0, b + 1)
                link0(nc.vector.tensor_copy(y_all[:, b * BLK:(b + 1) * BLK].rearrange("p (t c) -> p t c", c=C), y_blk))
            assert n0[0] == CHAIN0 * NBLK

            dve.wait_ge(s_ag, NBLK)
            nc.vector.memset(deg1_row, 1.0).then_inc(p1.chain, 1)
            dve.wait_ge(p1.chain, 1)
            dve.wait_ge(s_t1, NBLK)
            dve.sem_inc(p1.added, 2)
            dve.sem_inc(s_zc, 2)
            K = 4 * SLOTS
            with dve.Fori(0, end, NB) as c0:
                dve.wait_ge(s_win, end + c0 + 1)
                dve.sem_inc(s_gate)
                with dve.Fori(0, NB) as b:
                    c = c0 + b
                    for s in range(SLOTS):
                        make_onehot(b, s).then_inc(p1.onehot, 1)
                    for s in range(SLOTS):
                        def chained(ins, j):
                            ins.then_inc(p1.chain, 1)
                            dve.wait_ge(p1.chain, c * K + (4 * s + j + 1))

                        dve.wait_ge(s_z, c * SLOTS + (s + 1))
                        dve.wait_ge(p1.rows_full[s], (c + 1) * (16 * UNITS))
                        zs = z_edge[:, s, :, :]
                        nc.vector.tensor_tensor(
                            zs, psum[:, 4 + s % 2, :].rearrange("p (u h) -> p u h", h=H), rows[:, s, :, 0:H],
                            ALU.add).then_inc(s_zc, 1)
                        cols = dst_rel[:, dst_cols(b, s)]
                        chained(nc.vector.tensor_scalar(mask[:, s, :], cols, iota_cur[:, 0:1], 0.5,
                                                        ALU.is_ge, ALU.mult), 1)
                        chained(nc.vector.scalar_tensor_tensor(mask[:, s, :], cols, iota_cur[:, WIN - 1:WIN],
                                                               mask[:, s, :], ALU.is_le, ALU.mult), 2)
                        dve.wait_ge(s_gelu, c * SLOTS + (s + 1))
                        chained(nc.vector.tensor_tensor(zs, gelu_edge[:, s % 2, :, :], w2_all[:, 0:H].unsqueeze(1)
                                                        .to_broadcast([P, UNITS, H]), ALU.mult), 3)
                        nc.vector.tensor_reduce(logit[:, s, :], zs, AX, ALU.add).then_inc(s_log, 1)
                        w = window(b, s)
                        dve.wait_ge(s_tanh, c * SLOTS + (s + 1))
                        nc.vector.scalar_tensor_tensor(ew[:, s, :], tanh_edge[:, s, :], 1.0, mask[:, s, :],
                                                       ALU.add, ALU.mult).then_inc(s_ew, 1)
                        dve.wait_ge(s_ew, c * SLOTS + (s + 1))
                        at = ew_all[:, dst_cols(b, s)]
                        chained(nc.vector.tensor_tensor(at, at, ew[:, s, :], ALU.add), 4)
                        dve.wait_ge(p1.used, c * SLOTS + (s + 1 + SLOTS))
                        nc.vector.tensor_tensor(deg1_row[:, bass.ds(w, WIN)], deg1_row[:, bass.ds(w, WIN)],
                                                psum[0:1, 6 + s % 2, 0:WIN], ALU.add).then_inc(p1.added, 1)
                        dve.wait_ge(p1.added, c * SLOTS + (s + 3))
                next_round()
            end_pass(p1, 1)

            degree_tile(1).then_inc(s_dgn, 1)
            dve.wait_ge(s_dgn, 2)
            dve.wait_ge(s_rstd, NBLK + 1)
            for b in range(NBLK):
                if b:
                    dve.wait_ge(s_t2, 16 * b)
                    dve.wait_ge(s_s2t, b)
                nc.vector.tensor_tensor(
                    v_blk, y_all[:, b * BLK:(b + 1) * BLK].rearrange("p (t c) -> p t c", c=C),
                    degn[:, b * BT:(b + 1) * BT].unsqueeze(2).to_broadcast([P, BT, C]), ALU.mult).then_inc(s_s2, 1)
            dve.wait_ge(s_s2c, NBLK)
            dve.sem_inc(p2.added, SLOTS)
            sum_pass(p2, 2, False)

            n2 = [0]

            def link2(ins):
                n2[0] += 1
                ins.then_inc(s_v2, 1)
                dve.wait_ge(s_v2, n2[0])

            for b in range(NBLK):
                dve.wait_ge(s_c2, b + 1)
                o = (b % 2) * 1024
                link2(nc.vector.tensor_tensor(
                    v_blk, ps_flat[:, o:o + BLK].rearrange("p (t c) -> p t c", c=C),
                    degn[:, b * BT:(b + 1) * BT].unsqueeze(2).to_broadcast([P, BT, C]), ALU.mult))
                yb = y_all[:, b * BLK:(b + 1) * BLK].rearrange("p (t c) -> p t c", c=C)
                link2(nc.vector.tensor_tensor(v_blk, v_blk, yb, ALU.add))
                link2(nc.vector.tensor_tensor(v_blk, v_blk, conv_bias[:, :].unsqueeze(1).to_broadcast([P, BT, C]),
                                              ALU.add))
                layer_norm(link2, NBLK + 1 + b + 1)
                for t in range(BT):
                    last = nc.vector.tensor_scalar(yb[:, t, :], v_blk[:, t, :], mv[:, t, 0:1], rstd[:, t:t + 1],
                                                   ALU.subtract, ALU.mult)
                last.then_inc(s_zd, 1)
                dve.wait_ge(s_zd, b + 1)
            assert n2[0] == CHAIN2 * NBLK


_INS = ['x', 'src', 'dst', 'L0_gnn_W1', 'L0_gnn_b1', 'L0_gnn_W2', 'L1_gnn_mlp_w1', 'L1_gnn_mlp_b1',
        'L1_gnn_mlp_w2', 'L1_gnn_mlp_b2', 'L1_gnn_conv_w', 'L1_gnn_conv_b']


def kernel(**inputs):
    import numpy as _np
    import concourse.bacc as _bacc
    from concourse import mybir as _mybir
    from concourse.bass_utils import run_bass_kernel_spmd as _run

    nc = _bacc.Bacc("TRN2", target_bir_lowering=False, num_devices=1)
    arrays, args = {}, []
    for name in _INS:
        a = _np.ascontiguousarray(inputs[name])
        arrays[f"in_{name}_dram"] = a
        args.append(nc.dram_tensor(f"in_{name}_dram", a.shape, _mybir.dt.from_np(a.dtype), kind="ExternalInput").ap())
    shape = inputs["x"].shape
    args.append(nc.dram_tensor("out_0_dram", shape, _mybir.dt.float32, kind="ExternalOutput").ap())
    graph_kernel(nc, *args)
    r = _run(nc, [arrays], core_ids=[0])
    return r.results[0]["out_0_dram"]
```

```python
import concourse.bass as bass
from concourse import mybir
from concourse.alu_op_type import AluOpType as ALU
from contextlib import ExitStack

F32 = mybir.dt.float32
I32 = mybir.dt.int32
BF16 = mybir.dt.bfloat16
ACT = mybir.ActivationFunctionType
AX = mybir.AxisListType.X

P = 128
UNITS = 8
BATCH = P * UNITS
WIN = 64
AHEAD = 2
SLOTS = 4
BT = 7
BLK = BT * P
EPS = 1e-5


def graph_kernel(nc, x, src, dst, W1, b1, W2, mlp_w1, mlp_b1, mlp_w2, mlp_b2, conv_w, conv_b, out):
    N, C = x.shape
    E = src.shape[0]
    H = mlp_w1.shape[1]
    assert C == P and H == WIN
    ROW = H + C
    NBLK = -(-N // BLK)
    NT = NBLK * BT
    NPAD = NT * P
    COLS = NPAD + WIN
    assert NT <= P
    NG = -(-E // (BATCH * SLOTS)) * SLOTS
    NB = NG // SLOTS
    CH = -(-NG // P)
    FULL = E // BATCH
    REST = E - FULL * BATCH
    PAD_DST = 2 * COLS
    WIN_BITS = WIN.bit_length() - 1
    MAX_ROUNDS = NPAD // WIN + 1

    x_pad = nc.dram_tensor("x_pad", (NPAD, C), F32, kind="Internal").ap()
    table1 = nc.dram_tensor("table1", (NPAD, ROW), F32, kind="Internal").ap()
    edge_rows = nc.dram_tensor("edge_rows", (NG, P, UNITS * C), F32, kind="Internal").ap()
    src_lo = nc.dram_tensor("src_lo", (NG + AHEAD, BATCH), BF16, kind="Internal").ap()
    dst_part = nc.dram_tensor("dst_part", (COLS, H), F32, kind="Internal").ap()
    deg_lin = nc.dram_tensor("deg_lin", (2, NPAD), F32, kind="Internal").ap()

    ctx = ExitStack()
    with ctx:
        def sb(name, shape, dt=F32):
            return ctx.enter_context(nc.sbuf_tensor(name, shape, dt))

        def sem(name):
            return ctx.enter_context(nc.semaphore(name))

        def sems(name, n):
            return [sem(f"{name}{i}") for i in range(n)]

        acc = sb("acc", [P, COLS])
        y_all = sb("y_all", [P, COLS])
        meta = sb("meta", [P, 3, NG * UNITS])
        dst_rel, ew_all, src_hi = meta[:, 0, :], meta[:, 1, :], meta[:, 2, :]
        src_all = src_hi.bitcast(I32)
        rows = sb("rows", [P, SLOTS, UNITS, ROW])
        onehot = sb("onehot", [P, SLOTS, UNITS, WIN])
        idx = sb("idx", [P, SLOTS, UNITS], I32)
        win_base = sb("win_base", [1, NG], I32)
        win_cur = sb("win_cur", [1, NG], I32)
        iota_i = sb("iota_i", [P, WIN], I32)
        iota0 = sb("iota0", [P, WIN])
        iota_cur = sb("iota_cur", [P, WIN])
        ident = sb("ident", [P, P])
        ones = sb("ones", [P, P])
        gmin_t = sb("gmin_t", [P, CH])
        span_t = sb("span_t", [P, CH])
        span1 = sb("span1", [P, 1])
        rounds_i = sb("rounds_i", [1, 2], I32)
        w_raw = sb("w_raw", [P, 2, C])
        w_diff = sb("w_diff", [P, C])
        wd_t = sb("wd_t", [P, C])
        w2_t = sb("w2_t", [P, C])
        w_ab = sb("w_ab", [P, 2, H])
        cw = sb("cw", [P, C])
        bias = sb("bias", [P, 3, C])
        w2_row = sb("w2_row", [P, H + 1])
        dst_bias = sb("dst_bias", [P, H])
        conv_bias = sb("conv_bias", [P, C])
        minus_half = sb("minus_half", [P, NT])
        zeros = sb("zeros", [P, C])
        w2_all = sb("w2_all", [P, H + 1])
        deg_t = sb("deg_t", [P, P])
        degn = sb("degn", [P, NT])
        scratch = sb("scratch", [P, 5 * BLK])
        bn = sb("bn", [P, 2, BT, 6])
        mv = sb("mv", [P, 2, BT, 2])
        rstd = sb("rstd", [P, 2, BT])

        def blk(a):
            return a.rearrange("p (t c) -> p t c", t=BT)

        def x_blk(b):
            return blk(scratch[:, (b % 2) * BLK:(b % 2 + 1) * BLK])

        xt_blk = scratch[:, 2 * BLK:3 * BLK]
        yt_blk = scratch[:, 3 * BLK:4 * BLK]
        rows_flat = rows[:, :, :, :].rearrange("p s u c -> p (s u c)")
        v_place = onehot[:, :, :, :].rearrange("p s u w -> p (s u w)")

        def v_blk(b):
            return blk(v_place[:, (b % 2) * BLK:(b % 2 + 1) * BLK])

        def y_blk(b):
            return blk(scratch[:, 4 * BLK:5 * BLK]) if b % 2 else blk(rows_flat[:, 2 * BT * (ROW + H):2 * BT * (ROW + H) + BLK])

        def t1_blk(b):
            return blk(rows_flat[:, (b % 2) * BT * ROW:(b % 2 + 1) * BT * ROW])

        def d_blk(b):
            o = 2 * BT * ROW + (b % 2) * BT * H
            return blk(rows_flat[:, o:o + BT * H])

        assert 2 * BT * (ROW + H) + BLK <= SLOTS * UNITS * ROW and 2 * BLK <= SLOTS * UNITS * WIN
        z_edge = scratch[:, 0:SLOTS * UNITS * H].rearrange("p (s u h) -> p s u h", s=SLOTS, u=UNITS)
        o1 = SLOTS * UNITS * H
        oh_t = scratch[0:WIN, o1:o1 + 2 * BATCH].rearrange("w (b u p) -> w b u p", b=2, u=UNITS)
        gelu_edge = sb("gelu_edge", [P, 2, UNITS, H])
        d_win = sb("d_win", [WIN, SLOTS, H])
        logit = sb("logit", [P, SLOTS, UNITS])
        tanh_edge = sb("tanh_edge", [P, SLOTS, UNITS])
        mask = sb("mask", [P, SLOTS, UNITS])
        ew = sb("ew", [P, SLOTS, UNITS])
        lane = sb("lane", [P, 1])
        tile_no = sb("tile_no", [P, NT])
        lane_i = sb("lane_i", [P, 1], I32)
        tile_i = sb("tile_i", [P, NT], I32)
        dinv_parts = sb("dinv_parts", [P, 3, NT], BF16)
        dinv_rest = sb("dinv_rest", [P, NT])
        batch_meta = sb("batch_meta", [P, SLOTS, 3, UNITS])
        dinv_src = sb("dinv_src", [P, SLOTS, UNITS])
        weight = sb("weight", [P, SLOTS, UNITS])
        assert o1 + 2 * BATCH <= 5 * BLK

        rows2 = rows_flat[:, 0:SLOTS * UNITS * C].rearrange("p (s u c) -> p s u c", s=SLOTS, u=UNITS)
        lo_rows = scratch[:, 0:SLOTS * BATCH // 2].bitcast(BF16).rearrange("p (s e) -> p s e", s=SLOTS)
        lo_hot = scratch[:, SLOTS * BATCH // 2:(SLOTS + 2) * BATCH // 2].bitcast(BF16)\
            .rearrange("p (b e) -> p b e", b=2)
        o2 = (SLOTS + 2) * BATCH // 2
        picked = scratch[:, o2:o2 + UNITS * NT].rearrange("p (u t) -> p u t", u=UNITS)
        assert o2 + UNITS * NT <= 5 * BLK
        lo_all = ew_all[:, 0:CH * BATCH // 2].bitcast(BF16).rearrange("g (c e) -> g c e", c=CH)
        assert CH * BATCH // 2 <= NG * UNITS and (SLOTS + 2) * BATCH // 2 <= 5 * BLK

        raw_dst = y_all[:, 0:CH * BATCH].bitcast(I32).rearrange("g (c e) -> g c e", c=CH)
        raw_src = y_all[:, CH * BATCH:2 * CH * BATCH].bitcast(I32).rearrange("g (c e) -> g c e", c=CH)
        raw_f = acc[:, 0:CH * BATCH].rearrange("g (c e) -> g c e", c=CH)
        gmin = acc[:, CH * BATCH:CH * BATCH + NG]
        gmax = acc[:, CH * BATCH + NG:CH * BATCH + 2 * NG]
        capped = acc[:, CH * BATCH + 2 * NG:CH * BATCH + 2 * NG + NG * UNITS]
        base_f = y_all[:, 0:NG]
        assert CH * BATCH + 2 * NG + NG * UNITS <= COLS
        deg0_row = y_all[0:1, :]
        deg1_row = acc[0:1, :]

        psum = ctx.enter_context(nc.psum_tensor("psum", [P, 8, 512], F32))
        ps_flat = psum[:, :, :].rearrange("p b n -> p (b n)")

        s_w = sem("s_weights_loaded")
        s_dst = sem("s_dst_loaded")
        s_src = sem("s_src_loaded")
        s_xpad = sem("s_x_padded")
        s_iota = sem("s_iota")
        s_cst = sem("s_constants")
        s_pads = sem("s_pads_set")
        s_float = sem("s_indices_as_float")
        s_tr = sem("s_chunk_transposed")
        s_ev = sem("s_chunk_evacuated")
        s_pp = sem("s_prologue_product")
        s_pv = sem("s_prologue_vector")
        s_win = sem("s_windows_ready")
        s_zero = sem("s_zero_rows")
        s_gate = sem("s_gate")
        s_var = sem("s_variances_ready")
        s_rstd = sem("s_powers_ready")
        s_chain = sem("s_prologue_chain")
        CHAIN2 = 5

        class Pass:

            def __init__(self, name):
                self.idx_full = sems(f"{name}_idx_full", SLOTS)
                self.rows_full = sems(f"{name}_rows_full", SLOTS)
                self.onehot = sem(f"{name}_onehot_ready")
                self.used = sem(f"{name}_slot_used")
                self.added = sem(f"{name}_sums_added")
                self.chain = sem(f"{name}_vector_chain")
                self.done = sem(f"{name}_done")

        p0, p1, p2 = Pass("p0"), Pass("p1"), Pass("p2")
        s_dwin = sems("p1_dst_window_full", SLOTS)
        s_oht = sem("p1_onehot_transposed")
        s_ohc = sem("p1_transpose_copied")
        s_z = sem("p1_dst_product")
        s_zc = sem("p1_z_ready")
        s_gelu = sem("p1_gelu_ready")
        s_log = sem("p1_logit_ready")
        s_tanh = sem("p1_tanh_ready")
        s_ew = sem("p1_ew_ready")

        s_dg = sem("s_degree_row_stored")
        s_dgl = sem("s_degree_loaded")
        s_dgt = sem("s_degree_transposed")
        s_dgn = sem("s_degree_ready")
        s_lo = sem("s_source_lows_ready")
        s_los = sem("s_source_lows_stored")
        s_xb = sems("n0_x_block", 2)
        s_xt = sem("n0_x_transposed")
        s_xc = sem("n0_x_copied")
        s_uv = sem("n0_products")
        s_v0 = sem("n0_vector_chain")
        s_used0 = sem("n0_products_used")
        s_y0 = sem("n0_y_ready")
        s_yt = sem("n0_y_transposed")
        s_yc = sem("n0_y_copied")
        s_ab = sem("n0_table_product")
        s_ta = sem("n0_table_rows_from_scalar")
        s_td = sem("n0_dst_part_from_vector")
        s_ts = sems("n0_table_stored", 2)
        s_tds = sems("n0_dst_part_stored", 2)
        s_rs = sems("p1_rows_stored", SLOTS)
        s_s2 = sem("n1_scaled_ready")
        s_s2t = sem("n1_scaled_transposed")
        s_s2c = sem("n1_scaled_copied")
        s_parts = sem("n1_dinv_parts_ready")
        s_lof = sems("p2_source_lows_full", SLOTS)
        s_look = sem("p2_low_one_hot_ready")
        s_found = sem("p2_dinv_candidates_ready")
        s_sel = sem("p2_dinv_selected")
        s_meta = sem("p2_batch_meta_ready")
        s_c2 = sem("n2_products")
        s_v2 = sem("n2_vector_chain")
        s_zd = sem("n2_z_ready")
        s_out = sem("s_out_stored")

        block = ctx.enter_context(nc.Block())

        def load_rounds(eng):
            return eng.snap(eng.value_load(rounds_i[0:1, 0:1], min_val=1, max_val=MAX_ROUNDS) * NB)

        def sum_psum(s):
            return psum[:, s, 0:WIN], psum[0:1, s, WIN:2 * WIN]

        def candidates(q, u):
            return psum[:, 4 + 2 * q + u // 4, (u % 4) * NT:(u % 4 + 1) * NT]

        def degrees(sp, p, row, n):
            sp.wait_ge(p.done, 1)
            sp.dma_start(deg_lin[n:n + 1, :], row[:, 0:NPAD]).then_inc(s_dg, 16)
            sp.wait_ge(s_dg, 16 * (n + 1))
            sp.dma_start(deg_t[0:NT, :], deg_lin[n, :].rearrange("(t p) -> t p", p=P)).then_inc(s_dgl, 16)

        @block.sync
        def _(sp):
            sp.wait_ge(s_pads, 1)
            for raw, ind, done in ((raw_dst, dst, s_dst), (raw_src, src, s_src)):
                for c in range(CH):
                    lo, hi = c * P, min(FULL, (c + 1) * P)
                    if hi > lo:
                        sp.dma_start(raw[0:hi - lo, c, :],
                                     ind[lo * BATCH:hi * BATCH].rearrange("(g e) -> g e", e=BATCH)).then_inc(done, 16)
                if REST:
                    sp.dma_start(raw[FULL % P:FULL % P + 1, FULL // P, 0:REST],
                                 ind[FULL * BATCH:E].rearrange("(g e) -> g e", g=1)).then_inc(done, 16)
            for t, w in enumerate((W1, W2)):
                sp.dma_start(w_raw[:, t, :], w).then_inc(s_w, 16)
            sp.dma_start(w_ab[:, 0, :], mlp_w1[0:C, :]).then_inc(s_w, 16)
            sp.dma_start(w_ab[:, 1, :], mlp_w1[C:2 * C, :]).then_inc(s_w, 16)
            sp.dma_start(cw[:, :], conv_w).then_inc(s_w, 16)
            sp.wait_ge(s_cst, 1)
            sp.dma_start(bias[0:1, 0, :], b1.rearrange("(a n) -> a n", a=1)).then_inc(s_w, 16)
            sp.dma_start(bias[0:1, 1, H:2 * H], mlp_b1.rearrange("(a n) -> a n", a=1)).then_inc(s_w, 16)
            sp.dma_start(bias[0:1, 2, :], conv_b.rearrange("(a n) -> a n", a=1)).then_inc(s_w, 16)
            sp.dma_start(w2_row[0:1, 0:H], mlp_w2.rearrange("h a -> a h")).then_inc(s_w, 16)
            sp.dma_start(w2_row[0:1, H:H + 1], mlp_b2.rearrange("(a n) -> a n", a=1)).then_inc(s_w, 16)
            sp.dma_start(x_pad[0:N, :], x).then_inc(s_xpad, 16)
            for lo in range(N, NPAD, P):
                m = min(P, NPAD - lo)
                sp.dma_start(x_pad[lo:lo + m, :], zeros[0:m, :]).then_inc(s_xpad, 16)
            sp.dma_start(dst_part[NPAD:COLS, :], zeros[0:WIN, 0:H]).then_inc(s_zero, 16)
            sp.wait_ge(s_win, 1)
            end = load_rounds(sp)

            def load_idx(p, c, b, s):
                sp.wait_ge(p.used, c * SLOTS + (s + 1))
                at = b * (SLOTS * UNITS) + s * UNITS
                sp.dma_start(idx[:, s, :], src_all[:, bass.ds(at, UNITS)]).then_inc(p.idx_full[s], 16)

            with sp.Fori(0, end, NB) as c0:
                with sp.Fori(0, NB) as b:
                    c = c0 + b
                    for s in range(SLOTS):
                        load_idx(p0, c, b, s)
            degrees(sp, p0, deg0_row, 0)
            for b in range(NBLK):
                sp.wait_ge(s_ta, b + 1)
                sp.dma_start(table1[b * BLK:(b + 1) * BLK, :].rearrange("(t p) c -> p t c", p=P), t1_blk(b)).then_inc(s_ts[b % 2], 16)
                sp.wait_ge(s_td, b + 1)
                sp.dma_start(dst_part[b * BLK:(b + 1) * BLK, :].rearrange("(t p) c -> p t c", p=P), d_blk(b)).then_inc(s_tds[b % 2], 16)
            for q in range(2):
                sp.wait_ge(s_tds[q], 16 * ((NBLK + 1 - q) // 2))
            sp.wait_ge(s_zero, 16)
            with sp.Fori(0, end, NB) as c0:
                sp.wait_ge(s_win, end + c0 + 1)
                sp.sem_inc(s_gate)
                with sp.Fori(0, NB) as b:
                    c = c0 + b
                    for s in range(SLOTS):
                        load_idx(p1, c, b, s)
                        w = sp.value_load(win_cur[0:1, bass.ds(b * SLOTS + s, 1)], min_val=0, max_val=NPAD)
                        sp.dma_start(d_win[:, s, :], dst_part[bass.ds(w, WIN), :]).then_inc(s_dwin[s], 16)
            degrees(sp, p1, deg1_row, 1)
            sp.wait_ge(s_los, 16 * (CH + 1))

            def load_lows(row, s):
                sp.dma_start(lo_rows[:, s, :], src_lo[row, :].partition_broadcast(P)).then_inc(s_lof[s], 16)

            sp.wait_ge(s_s2c, NBLK)
            for j in range(AHEAD):
                load_lows(bass.ds(j, 1), j)
            with sp.Fori(0, end, NB) as c0:
                with sp.Fori(0, NB) as b:
                    c = c0 + b
                    for s in range(SLOTS):
                        sp.wait_ge(p2.used, c * SLOTS + (s + 1))
                        sp.dma_start(rows2[:, s, :, :].rearrange("p u c -> p (u c)"),
                                     edge_rows[bass.ds(b * SLOTS + s, 1), :, :].rearrange("a p n -> p (a n)"))\
                            .then_inc(p2.rows_full[s], 16)
                        sp.wait_ge(s_look, c * SLOTS + (s + AHEAD + 1))
                        load_lows(bass.ds(b * SLOTS + (s + AHEAD), 1), (s + AHEAD) % SLOTS)
            stores = 0
            for b in range(NBLK):
                sp.wait_ge(s_zd, b + 1)
                tiles = min(BT, max(0, (N - b * BLK) // P))
                lo = b * BLK
                if tiles:
                    sp.dma_start(out[lo:lo + tiles * P, :].rearrange("(t p) c -> p t c", p=P),
                                 y_all[:, lo:lo + tiles * P].rearrange("p (t c) -> p t c", c=C)).then_inc(s_out, 16)
                    stores += 1
                left = min(N - lo - tiles * P, P) if tiles < BT else 0
                if left > 0:
                    sp.dma_start(out[lo + tiles * P:lo + tiles * P + left, :],
                                 y_all[0:left, lo + tiles * P:lo + (tiles + 1) * P]).then_inc(s_out, 16)
                    stores += 1
            sp.wait_ge(s_out, 16 * stores)

        @block.gpsimd
        def _(pool):
            pool.iota(lane_i[:, :], pattern=[[0, 1]], base=0, channel_multiplier=1)
            pool.iota(tile_i[:, :], pattern=[[1, NT]], base=0, channel_multiplier=0)
            pool.iota(iota_i[:, :], pattern=[[1, WIN]], base=0, channel_multiplier=0).then_inc(s_iota, 1)
            pool.memset(ident[:, :], 0.0).then_inc(s_iota, 1)
            pool.wait_ge(s_iota, 2)
            pool.affine_select(out=ident[:, :], in_=ident[:, :], compare_op=ALU.not_equal, fill=1.0, base=0,
                               pattern=[[-1, P]], channel_multiplier=1).then_inc(s_iota, 1)
            pool.wait_ge(s_win, 1)
            end = load_rounds(pool)

            def gather(p, table, width):
                with pool.Fori(0, end) as c:
                    for s in range(SLOTS):
                        pool.wait_ge(p.idx_full[s], (c + 1) * 16)
                        pool.sem_inc(s_gate)
                        for u in range(UNITS):
                            pool.indirect_dma_start(
                                out=rows[:, s, u, 0:width], out_offset=None, in_=table,
                                in_offset=bass.IndirectOffsetOnAxis(idx[:, s, u:u + 1], 0)).then_inc(p.rows_full[s], 16)

            gather(p0, x, C)

            def load_x(b):
                pool.dma_start(x_blk(b), x_pad[b * BLK:(b + 1) * BLK, :].rearrange("(t p) c -> p t c", p=P))\
                    .then_inc(s_xb[b % 2], 16)

            def inverse_deviations(made):
                for b in range(NBLK):
                    pool.wait_ge(s_var, made + b + 1)
                    if made == 0 and b + 2 < NBLK:
                        load_x(b + 2)
                    nc.gpsimd.tensor_tensor(rstd[:, b % 2, :], rstd[:, b % 2, :], minus_half[:, 0:BT], ALU.pow).then_inc(s_rstd, 1)

            pool.wait_ge(s_xpad, 16 * (1 + -(-(NPAD - N) // P)))
            load_x(0)
            load_x(1)
            inverse_deviations(0)
            for q in range(2):
                pool.wait_ge(s_ts[q], 16 * ((NBLK + 1 - q) // 2))
            gather(p1, table1, ROW)
            pool.wait_ge(s_dgn, 2)
            nc.gpsimd.tensor_tensor(degn[:, :], degn[:, :], minus_half[:, :], ALU.pow).then_inc(s_rstd, 1)
            inverse_deviations(NBLK)

        @block.tensor
        def _(pe):
            pe.wait_ge(s_iota, 3)
            pe.wait_ge(s_cst, 1)
            n = 0
            for a in range(2):
                for c in range(CH):
                    pe.wait_ge(s_float, a * CH + c + 1)
                    for h in range(UNITS // 4):
                        if n >= 4:
                            pe.wait_ge(s_ev, n - 3)
                        for u in range(4):
                            q = 4 * h + u
                            last = nc.tensor.transpose(psum[:, n % 4, u * P:(u + 1) * P],
                                                       raw_f[:, c, q * P:(q + 1) * P], ident[:, :])
                        last.then_inc(s_tr, 1)
                        n += 1
            pe.wait_ge(s_pv, 1)
            for c in range(CH):
                m = min(P, NG - c * P)
                nc.tensor.transpose(psum[0:m, 4, c * P:(c + 1) * P], gmin[:, c * P:c * P + m], ident[:, :])
                last = nc.tensor.transpose(psum[0:m, 5, c * P:(c + 1) * P], gmax[:, c * P:c * P + m], ident[:, :])
            last.then_inc(s_pp, 1)
            pe.wait_ge(s_pv, 2)
            for c in range(CH):
                m = min(P, NG - c * P)
                nc.tensor.matmul(psum[:, 6, c * P:c * P + m], ones[0:m, :], raw_f[0:m, 0, c * P:c * P + m],
                                 start=True, stop=True)
            nc.tensor.transpose(psum[0:1, 7, 0:P], span1[:, :], ident[:, :]).then_inc(s_pp, 1)
            pe.wait_ge(s_pv, 3)
            nc.tensor.transpose(psum[:, 0, 0:P], w_diff[:, :], ident[:, :])
            nc.tensor.transpose(psum[:, 0, P:2 * P], w_raw[:, 1, :], ident[:, :])
            nc.tensor.matmul(psum[:, 0, 2 * P:2 * P + H + 1], ones[:, :], w2_row[:, :], start=True, stop=True)
            nc.tensor.matmul(psum[:, 1, 0:2 * C], ones[:, :], bias[:, 1:3, :].rearrange("p a c -> p (a c)"),
                             start=True, stop=True).then_inc(s_pp, 1)

            def load_end():
                pe.wait_ge(s_win, 1)
                return load_rounds(pe)

            end = load_end()
            pe.sem_inc(p0.used, SLOTS)

            def sums(p, c, s, deg):
                pe.wait_ge(p.rows_full[s], (c + 1) * (16 * UNITS))
                pe.wait_ge(p.onehot, c * SLOTS + (s + 1))
                pe.wait_ge(p.added, c * SLOTS + (s + 1))
                total, count = sum_psum(s)
                for u in range(UNITS):
                    last = nc.tensor.matmul(total, rows[:, s, u, 0:C], onehot[:, s, u, :],
                                            start=(u == 0), stop=(u == UNITS - 1))
                if deg:
                    for u in range(UNITS):
                        last = nc.tensor.matmul(count, ones[:, 0:1], onehot[:, s, u, :],
                                                start=(u == 0), stop=(u == UNITS - 1))
                last.then_inc(p.used, 1)

            with pe.Fori(0, end) as c:
                for s in range(SLOTS):
                    sums(p0, c, s, True)

            def degree_tile(n):
                pe.wait_ge(s_dgl, 16 * (n + 1))
                nc.tensor.transpose(psum[:, 7, 0:NT], deg_t[0:NT, :], ident[0:NT, 0:NT]).then_inc(s_dgt, 1)

            degree_tile(0)

            def node_products(b):
                pe.wait_ge(s_xb[b % 2], 16 * (b // 2 + 1))
                if b >= 2:
                    pe.wait_ge(s_yc, b - 1)
                for t in range(BT):
                    last = nc.tensor.transpose(ps_flat[:, t * P:(t + 1) * P], x_blk(b)[:, t, :], ident[:, :])
                last.then_inc(s_xt, 1)
                if b:
                    pe.wait_ge(s_used0, b)
                for t in range(BT):
                    nc.tensor.matmul(ps_flat[:, 2048 + t * P:2048 + (t + 1) * P],
                                     acc[:, b * BLK + t * P:b * BLK + (t + 1) * P], w2_t[:, :], start=True, stop=True)
                pe.wait_ge(s_xc, b + 1)
                for t in range(BT):
                    u_out = ps_flat[:, 1024 + t * P:1024 + (t + 1) * P]
                    nc.tensor.matmul(u_out, xt_blk[:, t * P:(t + 1) * P], wd_t[:, :], start=True, stop=False)
                    last = nc.tensor.matmul(u_out, ones[:, :], bias[:, 0, :], start=False, stop=True)
                last.then_inc(s_uv, 1)

            def table_products(b):
                pe.wait_ge(s_y0, b + 1)
                pe.wait_ge(s_xc, min(b + 2, NBLK))
                for t in range(BT):
                    last = nc.tensor.transpose(ps_flat[:, t * P:(t + 1) * P], y_blk(b)[:, t, :], ident[:, :])
                last.then_inc(s_yt, 1)
                pe.wait_ge(s_yc, b + 1)
                if b:
                    pe.wait_ge(s_ta, b)
                    pe.wait_ge(s_td, b)
                for t in range(BT):
                    last = nc.tensor.matmul(ps_flat[:, 3072 + t * P:3072 + (t + 1) * P], yt_blk[:, t * P:(t + 1) * P],
                                            w_ab[:, :, :].rearrange("p a h -> p (a h)"), start=True, stop=True)
                last.then_inc(s_ab, 1)

            node_products(0)
            for b in range(NBLK):
                if b + 1 < NBLK:
                    node_products(b + 1)
                table_products(b)
            pe.sem_inc(p1.used, SLOTS)

            def oh_psum(b):
                return ps_flat[0:WIN, b * 1024:(b + 1) * 1024]

            def turn(c, s):
                pe.wait_ge(p1.onehot, c * SLOTS + (s + 1))
                pe.wait_ge(s_ohc, c * SLOTS + (s + 1))
                pe.sem_inc(s_gate)
                for u in range(UNITS):
                    last = nc.tensor.transpose(oh_psum(s % 2)[:, u * P:(u + 1) * P], onehot[:, s, u, :], ident[:, :])
                last.then_inc(s_oht, 1)

            def dst_rows(c, s):
                pe.wait_ge(s_dwin[s], (c + 1) * 16)
                pe.wait_ge(s_ohc, c * SLOTS + (s + 3))
                pe.wait_ge(s_zc, c * SLOTS + (s + 1))
                for u in range(UNITS):
                    last = nc.tensor.matmul(psum[:, 4 + s % 2, u * H:(u + 1) * H], oh_t[:, s % 2, u, :],
                                            d_win[:, s, :], start=True, stop=True)
                last.then_inc(s_z, 1)

            def degree_sum(c, s):
                pe.wait_ge(s_ew, c * SLOTS + (s + 1))
                pe.wait_ge(p1.added, c * SLOTS + (s + 1))
                pe.wait_ge(s_rs[s], (c + 1) * 16)
                for u in range(UNITS):
                    last = nc.tensor.matmul(psum[0:1, 6 + s % 2, 0:WIN], ew[:, s, u:u + 1], onehot[:, s, u, :],
                                            start=(u == 0), stop=(u == UNITS - 1))
                last.then_inc(p1.used, 1)

            with pe.Fori(0, end) as c:
                turn(c, 0)
                turn(c, 1)
                dst_rows(c, 0)
                turn(c, 2)
                dst_rows(c, 1)
                turn(c, 3)
                for s in range(SLOTS):
                    if s + 2 < SLOTS:
                        dst_rows(c, s + 2)
                    degree_sum(c, s)

            degree_tile(1)
            for b in range(NBLK):
                pe.wait_ge(s_s2, b + 1)
                if b:
                    pe.wait_ge(s_s2c, b)
                for t in range(BT):
                    last = nc.tensor.transpose(ps_flat[:, t * P:(t + 1) * P], v_blk(b)[:, t, :], ident[:, :])
                last.then_inc(s_s2t, 1)
            pe.sem_inc(p2.used, SLOTS)
            pe.wait_ge(s_s2c, NBLK)
            pe.wait_ge(s_parts, 1)

            def look_up(c, s):
                q = (s + AHEAD) % 2
                pe.wait_ge(s_look, c * SLOTS + (s + AHEAD + 1 + SLOTS))
                pe.wait_ge(s_sel, c * SLOTS + (s + AHEAD + 1))
                for u in range(UNITS):
                    for k in range(3):
                        last = nc.tensor.matmul(candidates(q, u), lo_hot[:, q, u * P:(u + 1) * P],
                                                dinv_parts[:, k, :], start=(k == 0), stop=(k == 2))
                last.then_inc(s_found, 1)

            def weighted_sums(c, s):
                pe.wait_ge(p2.rows_full[s], (c + 1) * 16)
                pe.wait_ge(p2.onehot, c * SLOTS + (s + 1))
                pe.wait_ge(p2.added, c * SLOTS + (s + 1))
                for u in range(UNITS):
                    last = nc.tensor.matmul(sum_psum(s)[0], rows2[:, s, u, :], onehot[:, s, u, :],
                                            start=(u == 0), stop=(u == UNITS - 1))
                last.then_inc(p2.used, 1)

            for j in range(AHEAD):
                look_up(0, j - AHEAD)
            with pe.Fori(0, end) as c:
                for s in range(SLOTS):
                    look_up(c, s)
                    weighted_sums(c, s)

            for b in range(NBLK):
                if b == 0:
                    pe.wait_ge(p2.done, 1)
                if b >= 4:
                    pe.wait_ge(s_v2, CHAIN2 * (b - 4) + 1)
                for t in range(BT):
                    o = (b % 4) * 1024 + t * P
                    last = nc.tensor.matmul(ps_flat[:, o:o + P], acc[:, b * BLK + t * P:b * BLK + (t + 1) * P],
                                            cw[:, :], start=True, stop=True)
                last.then_inc(s_c2, 1)

        @block.scalar
        def _(act):
            act.wait_ge(s_win, 1)
            end = load_rounds(act)
            act.wait_ge(s_lo, 1)
            for c in range(CH):
                m = min(P, NG - c * P)
                act.dma_start(src_lo[c * P:c * P + m, :], lo_all[0:m, c, :]).then_inc(s_los, 16)
            act.dma_start(src_lo[NG:NG + AHEAD, :], lo_all[0:AHEAD, 0, :]).then_inc(s_los, 16)

            def copy_x(b):
                act.wait_ge(s_xt, b + 1)
                if b:
                    act.wait_ge(s_uv, b)
                nc.scalar.activation(xt_blk, ps_flat[:, 0:BLK], ACT.Copy).then_inc(s_xc, 1)

            copy_x(0)
            for b in range(NBLK):
                if b + 1 < NBLK:
                    copy_x(b + 1)
                act.wait_ge(s_yt, b + 1)
                if b:
                    act.wait_ge(s_ab, b)
                nc.scalar.activation(yt_blk, ps_flat[:, 0:BLK], ACT.Copy).then_inc(s_yc, 1)
                if b >= 2:
                    act.wait_ge(s_ts[b % 2], 16 * (b // 2))
                nc.scalar.activation(t1_blk(b)[:, :, H:ROW], y_blk(b), ACT.Copy)
                act.wait_ge(s_ab, b + 1)
                ab = ps_flat[:, 3072:3072 + BLK].rearrange("p (t c) -> p t c", c=C)
                nc.scalar.activation(t1_blk(b)[:, :, 0:H], ab[:, :, 0:H], ACT.Copy).then_inc(s_ta, 1)

            act.sem_inc(s_ohc, 2)
            with act.Fori(0, end, NB) as c0, act.Fori(0, NB) as b:
                c = c0 + b

                def copy_turned(s):
                    act.wait_ge(s_oht, c * SLOTS + (s + 1))
                    act.wait_ge(s_zc, c * SLOTS + (s + 1))
                    nc.scalar.activation(oh_t[:, s % 2, :, :].rearrange("w u p -> w (u p)"),
                                         ps_flat[0:WIN, (s % 2) * 1024:(s % 2 + 1) * 1024], ACT.Copy).then_inc(s_ohc, 1)

                def weigh(s):
                    act.wait_ge(s_zc, c * SLOTS + (s + 3))
                    nc.scalar.activation(gelu_edge[:, s % 2, :, :], z_edge[:, s, :, :], ACT.Gelu)\
                        .then_inc(s_gelu, 1)
                    act.dma_start(edge_rows[bass.ds(b * SLOTS + s, 1), :, :].rearrange("a p (u c) -> p (a u) c", c=C),
                                  rows[:, s, :, H:ROW]).then_inc(s_rs[s], 16)
                    act.wait_ge(s_log, c * SLOTS + (s + 1))
                    nc.scalar.activation(tanh_edge[:, s, :], logit[:, s, :], ACT.Tanh, scale=0.5,
                                         bias=w2_all[:, H:H + 1]).then_inc(s_tanh, 1)

                copy_turned(0)
                copy_turned(1)
                for s in range(SLOTS):
                    if s + 2 < SLOTS:
                        copy_turned(s + 2)
                    weigh(s)
            for b in range(NBLK):
                act.wait_ge(s_s2t, b + 1)
                nc.scalar.activation(acc[:, b * BLK:(b + 1) * BLK], ps_flat[:, 0:BLK], ACT.Copy).then_inc(s_s2c, 1)
            act.wait_ge(s_parts, 1)
            with act.Fori(0, end, NB) as c0, act.Fori(0, NB) as b:
                c = c0 + b
                for s in range(SLOTS):
                    act.wait_ge(p2.added, c * SLOTS + (s + 1))
                    nc.scalar.activation(batch_meta[:, s, :, :], meta[:, :, bass.ds(b * (SLOTS * UNITS) + s * UNITS, UNITS)],
                                         ACT.Copy).then_inc(s_meta, 1)

        @block.vector
        def _(dve):
            made = [0]

            def chain(ins, s=s_chain):
                made[0] += 1
                ins.then_inc(s, 1)
                dve.wait_ge(s, made[0])

            for c in range(FULL // P, CH):
                nc.vector.memset(raw_src[:, c, :], 0)
                nc.vector.memset(raw_dst[:, c, :], PAD_DST)
            nc.vector.memset(zeros[:, :], 0.0).then_inc(s_pads, 1)
            nc.vector.memset(ones[:, :], 1.0)
            nc.vector.memset(span_t[:, :], 0.0)
            nc.vector.memset(minus_half[:, :], -0.5)
            nc.vector.memset(w2_row[:, :], 0.0)
            nc.vector.memset(bias[:, :, :], 0.0).then_inc(s_cst, 1)
            loads = sum(1 for c in range(CH) if min(FULL, (c + 1) * P) > c * P) + (REST > 0)
            n = 0
            for a, (raw, done, to) in enumerate(((raw_dst, s_dst, dst_rel), (raw_src, s_src, src_all))):
                dve.wait_ge(done, 16 * loads)
                if a:
                    dve.wait_ge(s_tr, n)
                for c in range(CH):
                    nc.vector.tensor_copy(raw_f[:, c, :], raw[:, c, :]).then_inc(s_float, 1)
                for c in range(CH):
                    m = min(P, NG - c * P)
                    for h in range(UNITS // 4):
                        dve.wait_ge(s_tr, n + 1)
                        nc.vector.tensor_copy(
                            to.rearrange("p (g u) -> p u g", u=UNITS)[:, 4 * h:4 * h + 4, c * P:c * P + m],
                            psum[:, n % 4, :].rearrange("p (u g) -> p u g", u=4)[:, :, 0:m]).then_inc(s_ev, 1)
                        n += 1
                if a == 0:
                    dve.wait_ge(s_ev, n)
                    chain(nc.vector.tensor_scalar(capped, dst_rel, float(N - 1), None, ALU.min))
                    nc.vector.tensor_reduce(gmin, dst_rel.rearrange("p (g u) -> p g u", u=UNITS), AX, ALU.min)
                    nc.vector.tensor_reduce(gmax, capped.rearrange("p (g u) -> p g u", u=UNITS), AX, ALU.max)\
                        .then_inc(s_pv, 1)
            dve.wait_ge(s_pp, 1)
            for c in range(CH):
                m = min(P, NG - c * P)
                nc.vector.tensor_reduce(gmin_t[0:m, c:c + 1], psum[0:m, 4, c * P:(c + 1) * P], AX, ALU.min)
                chain(nc.vector.tensor_reduce(span_t[0:m, c:c + 1], psum[0:m, 5, c * P:(c + 1) * P], AX, ALU.max))
                nc.vector.tensor_tensor(span_t[0:m, c:c + 1], span_t[0:m, c:c + 1], gmin_t[0:m, c:c + 1], ALU.subtract)
                chain(nc.vector.tensor_scalar(raw_f[0:m, 0, c * P:c * P + m], ident[0:m, 0:m],
                                              gmin_t[0:m, c:c + 1], None, ALU.mult))
            nc.vector.tensor_reduce(span1[:, :], span_t[:, :], AX, ALU.max).then_inc(s_pv, 1)
            dve.wait_ge(s_pp, 2)
            chain(nc.vector.tensor_scalar(base_f, psum[:, 6, 0:NG], float(NPAD), None, ALU.min))
            nc.vector.tensor_copy(win_base[0:1, :], base_f[0:1, :])
            nc.vector.tensor_copy(win_cur[0:1, :], base_f[0:1, :])
            chain(nc.vector.tensor_tensor(dst_rel.rearrange("p (g u) -> p g u", u=UNITS),
                                          dst_rel.rearrange("p (g u) -> p g u", u=UNITS),
                                          base_f.unsqueeze(2).to_broadcast([P, NG, UNITS]), ALU.subtract))
            chain(nc.vector.tensor_reduce(span1[0:1, :], psum[0:1, 7, 0:P], AX, ALU.max))
            chain(nc.vector.tensor_scalar(span1[0:1, :], span1[0:1, :], float(WIN), None, ALU.add))
            chain(nc.vector.tensor_copy(rounds_i[0:1, 1:2], span1[0:1, :]))
            chain(nc.vector.tensor_scalar(rounds_i[0:1, 0:1], rounds_i[0:1, 1:2], WIN_BITS, None,
                                          ALU.logical_shift_right))
            dve.wait_ge(s_iota, 1)
            nc.vector.tensor_copy(iota0[:, :], iota_i[:, :])
            nc.vector.tensor_copy(iota_cur[:, :], iota_i[:, :])
            nc.vector.tensor_copy(lane[:, :], lane_i[:, :])
            nc.vector.tensor_copy(tile_no[:, :], tile_i[:, :])
            nc.vector.memset(acc[:, :], 0.0).then_inc(s_win, 1)
            chain(nc.vector.tensor_scalar(raw_src, raw_src, P - 1, None, ALU.bitwise_and))
            nc.vector.tensor_copy(lo_all, raw_src).then_inc(s_lo, 1)
            dve.wait_ge(s_lo, 1)
            nc.vector.memset(deg0_row, 0.0)
            dve.wait_ge(s_win, 1)
            dve.wait_ge(s_w, 160)
            nc.vector.tensor_tensor(w_diff[:, :], w_raw[:, 0, :], w_raw[:, 1, :], ALU.subtract).then_inc(s_pv, 1)
            dve.wait_ge(s_pp, 3)
            nc.vector.tensor_copy(wd_t[:, :], psum[:, 0, 0:P])
            nc.vector.tensor_copy(w2_t[:, :], psum[:, 0, P:2 * P])
            nc.vector.tensor_scalar(w2_all[:, H:H + 1], psum[:, 0, 2 * P + H:2 * P + H + 1], 0.5, None, ALU.mult)
            nc.vector.tensor_copy(dst_bias[:, :], psum[:, 1, H:2 * H])
            nc.vector.tensor_copy(conv_bias[:, :], psum[:, 1, C:2 * C])
            nc.vector.tensor_copy(w2_all[:, 0:H], psum[:, 0, 2 * P:2 * P + H]).then_inc(p0.added, SLOTS)

            end = load_rounds(dve)

            def dst_cols(b, s):
                return bass.ds(b * (SLOTS * UNITS) + s * UNITS, UNITS)

            def window(b, s):
                return dve.value_load(win_cur[0:1, bass.ds(b * SLOTS + s, 1)], min_val=0, max_val=NPAD)

            def make_onehot(b, s):
                return nc.vector.tensor_tensor(
                    onehot[:, s, :, :],
                    dst_rel[:, dst_cols(b, s)].unsqueeze(2).to_broadcast([P, UNITS, WIN]),
                    iota_cur[:, :].unsqueeze(1).to_broadcast([P, UNITS, WIN]), ALU.is_equal)

            def next_round():
                nc.vector.tensor_scalar(iota_cur[:, :], iota_cur[:, :], float(WIN), None, ALU.add)
                nc.vector.tensor_scalar(win_cur[:, :], win_cur[:, :], float(WIN), float(NPAD), ALU.add, ALU.min)\
                    .then_inc(s_win, NB)

            def end_pass(p, n):
                dve.wait_ge(s_win, end * (n + 1) + 1)
                nc.vector.tensor_copy(iota_cur[:, :], iota0[:, :])
                nc.vector.tensor_copy(win_cur[:, :], win_base[:, :]).then_inc(p.done, 1)
                dve.wait_ge(p.done, 1)

            with dve.Fori(0, end, NB) as c0:
                dve.wait_ge(s_win, c0 + 1)
                dve.sem_inc(s_gate)
                with dve.Fori(0, NB) as b:
                    c = c0 + b
                    for s in range(SLOTS):
                        make_onehot(b, s).then_inc(p0.onehot, 1)
                    for s in range(SLOTS):
                        w = window(b, s)
                        dve.wait_ge(p0.used, c * SLOTS + (s + 1 + SLOTS))
                        dve.wait_ge(p0.added, c * SLOTS + (s + SLOTS))
                        total, count = sum_psum(s)
                        nc.vector.tensor_tensor(acc[:, bass.ds(w, WIN)], acc[:, bass.ds(w, WIN)], total, ALU.add)
                        nc.vector.tensor_tensor(deg0_row[:, bass.ds(w, WIN)], deg0_row[:, bass.ds(w, WIN)], count,
                                                ALU.add).then_inc(p0.added, 1)
                next_round()
            end_pass(p0, 0)

            def degree_tile(n):
                dve.wait_ge(s_dgt, n + 1)
                return nc.vector.tensor_copy(degn[:, :], psum[:, 7, 0:NT])

            degree_tile(0).then_inc(s_dgn, 1)
            dve.wait_ge(s_dgn, 1)

            n0 = [0]

            def link0(ins):
                n0[0] += 1
                ins.then_inc(s_v0, 1)
                dve.wait_ge(s_v0, n0[0])

            def residual0(b):
                v, q = v_blk(b), b % 2
                dve.wait_ge(s_uv, b + 1)
                u_ps, v_ps = blk(ps_flat[:, 1024:1024 + BLK]), blk(ps_flat[:, 2048:2048 + BLK])
                link0(nc.vector.tensor_tensor(v, u_ps, degn[:, b * BT:(b + 1) * BT].unsqueeze(2)
                                              .to_broadcast([P, BT, C]), ALU.mult))
                link0(nc.vector.tensor_tensor(v, v, v_ps, ALU.add))
                nc.vector.tensor_tensor(v, v, x_blk(b), ALU.add).then_inc(s_used0, 1)
                dve.wait_ge(s_used0, b + 1)
                normal_statistics(v, q, link0)

            def normal_statistics(v, q, link):
                for t in range(BT):
                    last = nc.vector.bn_stats(bn[:, q, t, :], v[:, t, :])
                link(last)
                for t in range(BT):
                    last = nc.vector.bn_aggr(mv[:, q, t, :], bn[:, q, t, :])
                link(last)
                nc.vector.tensor_scalar(rstd[:, q, :], mv[:, q, :, 1:2].rearrange("p t a -> p (t a)"), EPS, None,
                                        ALU.add).then_inc(s_var, 1)

            def normalise(v, q, made, to):
                dve.wait_ge(s_rstd, made)
                for t in range(BT):
                    last = nc.vector.tensor_scalar(to[:, t, :], v[:, t, :], mv[:, q, t, 0:1], rstd[:, q, t:t + 1],
                                                   ALU.subtract, ALU.mult)
                return last

            def finish0(b):
                if b >= 2:
                    dve.wait_ge(s_ta, b - 1)
                    dve.wait_ge(s_yt, b - 1)
                normalise(v_blk(b), b % 2, b + 1, y_blk(b)).then_inc(s_y0, 1)
                dve.wait_ge(s_y0, b + 1)
                nc.vector.tensor_copy(blk(y_all[:, b * BLK:(b + 1) * BLK]), y_blk(b))

            def finish_dst(b):
                dve.wait_ge(s_ta, b + 1)
                if b >= 2:
                    dve.wait_ge(s_tds[b % 2], 16 * (b // 2))
                nc.vector.tensor_tensor(d_blk(b), blk(ps_flat[:, 3072:3072 + BLK])[:, :, H:2 * H],
                                        dst_bias[:, :].unsqueeze(1).to_broadcast([P, BT, H]), ALU.add).then_inc(s_td, 1)

            residual0(0)
            for b in range(NBLK):
                if b:
                    finish_dst(b - 1)
                if b + 1 < NBLK:
                    residual0(b + 1)
                finish0(b)
            finish_dst(NBLK - 1)

            dve.wait_ge(s_los, 16 * (CH + 1))
            nc.vector.memset(ew_all, 0.0)
            nc.vector.memset(deg1_row, 1.0).then_inc(p1.chain, 1)
            dve.wait_ge(p1.chain, 1)
            dve.wait_ge(s_ta, NBLK)
            dve.sem_inc(p1.added, 2)
            dve.sem_inc(s_zc, 2)
            K = 4 * SLOTS
            with dve.Fori(0, end, NB) as c0:
                dve.wait_ge(s_win, end + c0 + 1)
                dve.sem_inc(s_gate)
                with dve.Fori(0, NB) as b:
                    c = c0 + b
                    for s in range(SLOTS):
                        make_onehot(b, s).then_inc(p1.onehot, 1)
                    for s in range(SLOTS):
                        def chained(ins, j):
                            ins.then_inc(p1.chain, 1)
                            dve.wait_ge(p1.chain, c * K + (4 * s + j + 1))

                        dve.wait_ge(s_z, c * SLOTS + (s + 1))
                        dve.wait_ge(p1.rows_full[s], (c + 1) * (16 * UNITS))
                        zs = z_edge[:, s, :, :]
                        nc.vector.tensor_tensor(
                            zs, psum[:, 4 + s % 2, :].rearrange("p (u h) -> p u h", h=H), rows[:, s, :, 0:H],
                            ALU.add).then_inc(s_zc, 1)
                        cols = dst_rel[:, dst_cols(b, s)]
                        chained(nc.vector.tensor_scalar(mask[:, s, :], cols, iota_cur[:, 0:1], 0.5,
                                                        ALU.is_ge, ALU.mult), 1)
                        chained(nc.vector.scalar_tensor_tensor(mask[:, s, :], cols, iota_cur[:, WIN - 1:WIN],
                                                               mask[:, s, :], ALU.is_le, ALU.mult), 2)
                        dve.wait_ge(s_gelu, c * SLOTS + (s + 1))
                        chained(nc.vector.tensor_tensor(zs, gelu_edge[:, s % 2, :, :], w2_all[:, 0:H].unsqueeze(1)
                                                        .to_broadcast([P, UNITS, H]), ALU.mult), 3)
                        nc.vector.tensor_reduce(logit[:, s, :], zs, AX, ALU.add).then_inc(s_log, 1)
                        w = window(b, s)
                        dve.wait_ge(s_tanh, c * SLOTS + (s + 1))
                        nc.vector.scalar_tensor_tensor(ew[:, s, :], tanh_edge[:, s, :], 1.0, mask[:, s, :],
                                                       ALU.add, ALU.mult).then_inc(s_ew, 1)
                        dve.wait_ge(s_ew, c * SLOTS + (s + 1))
                        at = ew_all[:, dst_cols(b, s)]
                        chained(nc.vector.tensor_tensor(at, at, ew[:, s, :], ALU.add), 4)
                        dve.wait_ge(p1.used, c * SLOTS + (s + 1 + SLOTS))
                        nc.vector.tensor_tensor(deg1_row[:, bass.ds(w, WIN)], deg1_row[:, bass.ds(w, WIN)],
                                                psum[0:1, 6 + s % 2, 0:WIN], ALU.add).then_inc(p1.added, 1)
                        dve.wait_ge(p1.added, c * SLOTS + (s + 3))
                next_round()
            end_pass(p1, 1)

            degree_tile(1).then_inc(s_dgn, 1)
            dve.wait_ge(s_dgn, 2)
            dve.wait_ge(s_rstd, NBLK + 1)
            rest = dinv_rest[:, :]
            for k in range(3):
                part = dinv_parts[:, k, :]
                chain(nc.vector.tensor_copy(part, degn[:, :] if k == 0 else rest))
                if k < 2:
                    chain(nc.vector.tensor_tensor(rest, degn[:, :] if k == 0 else rest, part, ALU.subtract))
            chain(nc.vector.tensor_scalar(src_all, src_all, P.bit_length() - 1, None, ALU.logical_shift_right))
            nc.vector.tensor_copy(src_hi, src_all).then_inc(s_parts, 1)
            for b in range(NBLK):
                if b >= 2:
                    dve.wait_ge(s_s2t, b - 1)
                nc.vector.tensor_tensor(
                    v_blk(b), blk(y_all[:, b * BLK:(b + 1) * BLK]),
                    degn[:, b * BT:(b + 1) * BT].unsqueeze(2).to_broadcast([P, BT, C]), ALU.mult).then_inc(s_s2, 1)
            dve.wait_ge(s_s2c, NBLK)
            dve.sem_inc(p2.added, SLOTS)
            dve.sem_inc(s_look, SLOTS)
            dve.sem_inc(s_sel, 2)

            def low_one_hot(c, s):
                at = (s + AHEAD) % SLOTS
                dve.wait_ge(s_lof[at], (c + (1 + (s + AHEAD) // SLOTS)) * 16)
                nc.vector.tensor_scalar(lo_hot[:, (s + AHEAD) % 2, :], lo_rows[:, at, :], lane[:, :], None,
                                        ALU.is_equal).then_inc(s_look, 1)

            def select(c, s):
                dve.wait_ge(s_meta, c * SLOTS + (s + 1))
                dve.wait_ge(s_found, c * SLOTS + (s + 1))
                for u in range(UNITS):
                    last = nc.vector.scalar_tensor_tensor(
                        picked[:, u, :], tile_no[:, :], batch_meta[:, s, 2, u:u + 1], candidates(s % 2, u),
                        ALU.is_equal, ALU.mult, accum_out=dinv_src[:, s, u:u + 1])
                last.then_inc(s_sel, 1)

            def weigh(c, s):
                dve.wait_ge(s_sel, c * SLOTS + (s + 3))
                nc.vector.tensor_tensor(weight[:, s, :], dinv_src[:, s, :], batch_meta[:, s, 1, :], ALU.mult)\
                    .then_inc(p2.chain, 1)
                dve.wait_ge(p2.chain, c * SLOTS + (s + 1))
                for u in range(UNITS):
                    last = nc.vector.tensor_scalar(onehot[:, s, u, :], iota_cur[:, :], batch_meta[:, s, 0, u:u + 1],
                                                   weight[:, s, u:u + 1], ALU.is_equal, ALU.mult)
                last.then_inc(p2.onehot, 1)

            def add_sums(c, b, s):
                w = window(b, s)
                dve.wait_ge(p2.used, c * SLOTS + (s + 1 + SLOTS))
                dve.wait_ge(p2.added, c * SLOTS + (s + SLOTS))
                nc.vector.tensor_tensor(acc[:, bass.ds(w, WIN)], acc[:, bass.ds(w, WIN)], sum_psum(s)[0],
                                        ALU.add).then_inc(p2.added, 1)

            for j in range(AHEAD):
                low_one_hot(0, j - AHEAD)
            with dve.Fori(0, end, NB) as c0:
                dve.wait_ge(s_win, end * 2 + c0 + 1)
                dve.sem_inc(s_gate)
                with dve.Fori(0, NB) as b:
                    c = c0 + b
                    for s in range(SLOTS):
                        select(c, s)
                        low_one_hot(c, s)
                        weigh(c, s)
                        if s:
                            add_sums(c, b, s - 1)
                    add_sums(c, b, SLOTS - 1)
                next_round()
            end_pass(p2, 2)

            n2 = [0]

            def link2(ins):
                n2[0] += 1
                ins.then_inc(s_v2, 1)
                dve.wait_ge(s_v2, n2[0])

            def residual2(b):
                v = v_blk(b)
                if b >= 2:
                    dve.wait_ge(s_zd, b - 1)
                dve.wait_ge(s_c2, b + 1)
                o = (b % 4) * 1024
                link2(nc.vector.tensor_tensor(
                    v, blk(ps_flat[:, o:o + BLK]),
                    degn[:, b * BT:(b + 1) * BT].unsqueeze(2).to_broadcast([P, BT, C]), ALU.mult))
                link2(nc.vector.tensor_tensor(v, v, blk(y_all[:, b * BLK:(b + 1) * BLK]), ALU.add))
                link2(nc.vector.tensor_tensor(v, v, conv_bias[:, :].unsqueeze(1).to_broadcast([P, BT, C]), ALU.add))
                normal_statistics(v, b % 2, link2)

            residual2(0)
            for b in range(NBLK):
                if b + 1 < NBLK:
                    residual2(b + 1)
                normalise(v_blk(b), b % 2, NBLK + 1 + b + 1, blk(y_all[:, b * BLK:(b + 1) * BLK])).then_inc(s_zd, 1)
            assert n2[0] == CHAIN2 * NBLK


_INS = ['x', 'src', 'dst', 'L0_gnn_W1', 'L0_gnn_b1', 'L0_gnn_W2', 'L1_gnn_mlp_w1', 'L1_gnn_mlp_b1',
        'L1_gnn_mlp_w2', 'L1_gnn_mlp_b2', 'L1_gnn_conv_w', 'L1_gnn_conv_b']


def kernel(**inputs):
    import numpy as _np
    import concourse.bacc as _bacc
    from concourse import mybir as _mybir
    from concourse.bass_utils import run_bass_kernel_spmd as _run

    nc = _bacc.Bacc("TRN2", target_bir_lowering=False, num_devices=1)
    arrays, args = {}, []
    for name in _INS:
        a = _np.ascontiguousarray(inputs[name])
        arrays[f"in_{name}_dram"] = a
        args.append(nc.dram_tensor(f"in_{name}_dram", a.shape, _mybir.dt.from_np(a.dtype), kind="ExternalInput").ap())
    shape = inputs["x"].shape
    args.append(nc.dram_tensor("out_0_dram", shape, _mybir.dt.float32, kind="ExternalOutput").ap())
    graph_kernel(nc, *args)
    r = _run(nc, [arrays], core_ids=[0])
    return r.results[0]["out_0_dram"]
```

```python
import concourse.bass as bass
from concourse import mybir
from concourse.alu_op_type import AluOpType as ALU
from contextlib import ExitStack

F32 = mybir.dt.float32
I32 = mybir.dt.int32
BF16 = mybir.dt.bfloat16
ACT = mybir.ActivationFunctionType
AX = mybir.AxisListType.X

P = 128
UNITS = 8
BATCH = P * UNITS
WIN = 40
STEP = 32
AHEAD = 2
KEPT = 5
KEPT_EDGES = P * KEPT
SLOTS = 4
BT = 7
BLK = BT * P
STATS = 4
EPS = 1e-5


def graph_kernel(nc, x, src, dst, W1, b1, W2, mlp_w1, mlp_b1, mlp_w2, mlp_b2, conv_w, conv_b, out):
    N, C = x.shape
    E = src.shape[0]
    H = mlp_w1.shape[1]
    assert C == P and STEP <= WIN
    ROW = H + C
    NBLK = -(-N // BLK)
    NT = NBLK * BT
    NPAD = NT * P
    COLS = NPAD + WIN
    assert NT <= P
    NG = -(-E // (BATCH * SLOTS)) * SLOTS
    NB = NG // SLOTS
    CH = -(-NG // P)
    FULL = E // BATCH
    REST = E - FULL * BATCH
    PAD_DST = 2 * COLS
    MAX_ROUNDS = NPAD // STEP + 1

    assert NT <= NB
    XPAD = NB * P

    x_pad = nc.dram_tensor("x_pad", (XPAD, C), F32, kind="Internal").ap()
    x_part = nc.dram_tensor("x_part", (XPAD, C), F32, kind="Internal").ap()
    table1 = nc.dram_tensor("table1", (NPAD, ROW), F32, kind="Internal").ap()
    edge_rows = nc.dram_tensor("edge_rows", (NG, P, KEPT * C), F32, kind="Internal").ap()
    src_lo = nc.dram_tensor("src_lo", (NG + AHEAD, KEPT_EDGES), BF16, kind="Internal").ap()
    table2 = nc.dram_tensor("table2", (NPAD, C), F32, kind="Internal").ap()
    dst_part = nc.dram_tensor("dst_part", (COLS, H), F32, kind="Internal").ap()
    deg_lin = nc.dram_tensor("deg_lin", (2, NPAD), F32, kind="Internal").ap()

    ctx = ExitStack()
    with ctx:
        def sb(name, shape, dt=F32):
            return ctx.enter_context(nc.sbuf_tensor(name, shape, dt))

        def sem(name):
            return ctx.enter_context(nc.semaphore(name))

        def sems(name, n):
            return [sem(f"{name}{i}") for i in range(n)]

        acc = sb("acc", [P, COLS])
        y_all = sb("y_all", [P, COLS])
        meta = sb("meta", [P, 3, (NG + AHEAD) * UNITS])
        dst_rel, ew_all, src_hi = (meta[:, k, 0:NG * UNITS] for k in range(3))
        meta_next_round = meta[:, :, NG * UNITS:(NG + AHEAD) * UNITS]
        src_all = src_hi.bitcast(I32)
        rows = sb("rows", [P, SLOTS, UNITS, ROW])
        v_place = sb("v_place", [P, 2 * BLK])
        onehot = v_place[:, 0:SLOTS * UNITS * WIN].rearrange("p (s u w) -> p s u w", s=SLOTS, u=UNITS)
        idx = sb("idx", [P, SLOTS, UNITS], I32)
        win_base = sb("win_base", [1, NG], I32)
        win_cur = sb("win_cur", [1, NG], I32)
        iota_i = sb("iota_i", [P, WIN], I32)
        iota0 = sb("iota0", [P, WIN])
        iota_cur = sb("iota_cur", [P, WIN])
        ident = sb("ident", [P, P])
        ones = sb("ones", [P, P])
        gmin_t = sb("gmin_t", [P, CH])
        span_t = sb("span_t", [P, CH])
        span1 = sb("span1", [P, 1])
        rounds_i = sb("rounds_i", [1, 2], I32)
        w_raw = sb("w_raw", [P, 2, C])
        w_diff = sb("w_diff", [P, C])
        wd_t = sb("wd_t", [P, C])
        w2_t = sb("w2_t", [P, C])
        w_ab = sb("w_ab", [P, 2, H])
        cw = sb("cw", [P, C])
        bias = sb("bias", [P, 3, C])
        w2_row = sb("w2_row", [P, H + 1])
        dst_bias = sb("dst_bias", [P, H])
        conv_bias = sb("conv_bias", [P, C])
        minus_half = sb("minus_half", [P, NT])
        zeros = sb("zeros", [P, C])
        w2_all = sb("w2_all", [P, H + 1])
        deg_t = sb("deg_t", [P, P])
        degn = sb("degn", [P, NT])
        scratch = sb("scratch", [P, 5 * BLK])
        bn = sb("bn", [P, STATS, BT, 6])
        mv = sb("mv", [P, STATS, BT, 2])
        rstd = sb("rstd", [P, STATS, BT])

        def blk(a):
            return a.rearrange("p (t c) -> p t c", t=BT)

        def x_blk(b):
            return blk(scratch[:, (b % 2) * BLK:(b % 2 + 1) * BLK])

        def u_blk(b):
            return blk(scratch[:, (2 + b % 2) * BLK:(3 + b % 2) * BLK])

        yt_blk = scratch[:, 4 * BLK:5 * BLK]
        x_tile, xt_tile, u_tile = (scratch[:, k * C:(k + 1) * C] for k in range(3))
        rows_flat = rows[:, :, :, :].rearrange("p s u c -> p (s u c)")

        def v_blk(b):
            return blk(v_place[:, (b % 2) * BLK:(b % 2 + 1) * BLK])

        TURNS = 8

        def dy_blk(b):
            k = b % TURNS
            return v_blk(k) if k < 2 else blk(rows_flat[:, (k - 2) * BLK:(k - 1) * BLK])

        assert STATS <= TURNS

        def t1_blk(b):
            return blk(rows_flat[:, (b % 2) * BT * ROW:(b % 2 + 1) * BT * ROW])

        def d_blk(b):
            o = 2 * BT * ROW + (b % 2) * BT * H
            return blk(rows_flat[:, o:o + BT * H])

        assert 2 * BT * (ROW + H) <= SLOTS * UNITS * ROW and SLOTS * UNITS * WIN <= 2 * BLK
        assert (TURNS - 2) * BLK <= SLOTS * UNITS * ROW
        z_edge = scratch[:, 0:SLOTS * UNITS * H].rearrange("p (s u h) -> p s u h", s=SLOTS, u=UNITS)
        o1 = SLOTS * UNITS * H
        oh_t = scratch[0:WIN, o1:o1 + 2 * BATCH].rearrange("w (b u p) -> w b u p", b=2, u=UNITS)
        gelu_edge = sb("gelu_edge", [P, 2, UNITS, H])
        d_win = sb("d_win", [WIN, SLOTS, H])
        logit = sb("logit", [P, SLOTS, UNITS])
        tanh_edge = sb("tanh_edge", [P, SLOTS, UNITS])
        mask = sb("mask", [P, SLOTS, UNITS])
        ew = sb("ew", [P, SLOTS, UNITS])
        lane = sb("lane", [P, 1])
        tile_no = sb("tile_no", [P, NT])
        lane_i = sb("lane_i", [P, 1], I32)
        tile_i = scratch[:, 0:NT].bitcast(I32)
        dinv_parts = sb("dinv_parts", [P, 3, NT], BF16)
        dinv_rest = sb("dinv_rest", [P, NT])
        kept_meta = sb("kept_meta", [P, SLOTS, 2, KEPT])
        dinv_src = sb("dinv_src", [P, SLOTS, KEPT])
        weight = sb("weight", [P, SLOTS, UNITS])
        minus_mean = sb("minus_mean", [P, STATS, BT])
        assert o1 + 2 * BATCH <= 5 * BLK

        rows2 = rows_flat[:, 0:SLOTS * UNITS * C].rearrange("p (s u c) -> p s u c", s=SLOTS, u=UNITS)
        o2 = SLOTS * KEPT_EDGES // 2
        o3 = o2 + KEPT_EDGES
        lo_rows = scratch[:, 0:o2].bitcast(BF16).rearrange("p (s e) -> p s e", s=SLOTS)
        lo_hot = scratch[:, o2:o3].bitcast(BF16).rearrange("p (b e) -> p b e", b=2)
        picked = scratch[:, o3:o3 + KEPT * NT].rearrange("p (u t) -> p u t", u=KEPT)
        o4 = o3 + KEPT * NT
        sums_sb = scratch[0:WIN, o4:o4 + 2 * C].rearrange("w (b c) -> w b c", b=2)
        assert o4 + 2 * C <= 5 * BLK
        lo_all = ew_all[:, 0:CH * BATCH // 2].bitcast(BF16).rearrange("g (c e) -> g c e", c=CH)
        assert CH * BATCH // 2 <= NG * UNITS

        raw_dst = y_all[:, 0:CH * BATCH].bitcast(I32).rearrange("g (c e) -> g c e", c=CH)
        raw_src = y_all[:, CH * BATCH:2 * CH * BATCH].bitcast(I32).rearrange("g (c e) -> g c e", c=CH)
        raw_f = acc[:, 0:CH * BATCH].rearrange("g (c e) -> g c e", c=CH)
        gmin = acc[:, CH * BATCH:CH * BATCH + NG]
        gmax = acc[:, CH * BATCH + NG:CH * BATCH + 2 * NG]
        capped = acc[:, CH * BATCH + 2 * NG:CH * BATCH + 2 * NG + NG * UNITS]
        base_f = y_all[:, 0:NG]
        assert CH * BATCH + 2 * NG + NG * UNITS <= COLS
        deg0_row = y_all[0:1, :]
        deg1_row = acc[0:1, :]

        psum = ctx.enter_context(nc.psum_tensor("psum", [P, 8, 512], F32))
        ps_flat = psum[:, :, :].rearrange("p b n -> p (b n)")

        s_w = sem("s_weights_loaded")
        s_dst = sem("s_dst_loaded")
        s_src = sem("s_src_loaded")
        s_xpad = sem("s_x_padded")
        s_iota = sem("s_iota")
        s_cst = sem("s_constants")
        s_pads = sem("s_pads_set")
        s_float = sem("s_indices_as_float")
        s_tr = sem("s_chunk_transposed")
        s_ev = sem("s_chunk_evacuated")
        s_pp = sem("s_prologue_product")
        s_pv = sem("s_prologue_vector")
        s_win = sem("s_windows_ready")
        s_clear = sem("s_sums_cleared")
        s_zero = sem("s_zero_rows")
        s_gate = sem("s_gate")
        s_var = sem("s_variances_ready")
        s_rstd = sem("s_powers_ready")
        s_chain = sem("s_prologue_chain")
        CHAIN2 = 3

        class Pass:

            def __init__(self, name):
                self.idx_full = sems(f"{name}_idx_full", SLOTS)
                self.rows_full = sems(f"{name}_rows_full", SLOTS)
                self.onehot = sem(f"{name}_onehot_ready")
                self.used = sem(f"{name}_slot_used")
                self.added = sem(f"{name}_sums_added")
                self.chain = sem(f"{name}_vector_chain")
                self.done = sem(f"{name}_done")

        p0, p1, p2 = Pass("p0"), Pass("p1"), Pass("p2")
        s_dwin = sems("p1_dst_window_full", SLOTS)
        s_oht = sem("p1_onehot_transposed")
        s_ohc = sem("p1_transpose_copied")
        s_z = sem("p1_dst_product")
        s_zc = sem("p1_z_ready")
        s_gelu = sem("p1_gelu_ready")
        s_log = sem("p1_logit_ready")
        s_tanh = sem("p1_tanh_ready")
        s_ew = sem("p1_ew_ready")

        s_dg = sem("s_degree_row_stored")
        s_dgl = sem("s_degree_loaded")
        s_dgt = sem("s_degree_transposed")
        s_dgn = sem("s_degree_ready")
        s_lo = sem("s_source_lows_ready")
        s_los = sem("s_source_lows_stored")
        s_xb = sems("n0_x_block", 2)
        s_tile = sem("p0_x_tile_full")
        s_tt = sem("p0_x_tile_transposed")
        s_tc = sem("p0_x_tile_copied")
        s_tu = sem("p0_x_tile_product")
        s_to = sem("p0_x_part_ready")
        s_tst = sem("p0_x_part_stored")
        s_prep = sem("n0_x_terms_ready")
        s_uv = sem("n0_products")
        s_v0 = sem("n0_vector_chain")
        s_used0 = sem("n0_products_used")
        s_nm0 = sem("n0_minus_mean_ready")
        s_y0 = sem("n0_y_ready")
        s_yt = sem("n0_y_transposed")
        s_yc = sem("n0_y_copied")
        s_ab = sem("n0_table_product")
        s_ta = sem("n0_table_rows_from_scalar")
        s_td = sem("n0_dst_part_from_vector")
        s_ts = sems("n0_table_stored", 2)
        s_tds = sems("n0_dst_part_stored", 2)
        s_rs = sems("p1_rows_stored", SLOTS)
        s_s2 = sem("n1_scaled_ready")
        s_s2t = sem("n1_scaled_transposed")
        s_s2c = sem("n1_scaled_copied")
        s_parts = sem("n1_dinv_parts_ready")
        s_lof = sems("p2_source_lows_full", SLOTS)
        s_look = sem("p2_low_one_hot_ready")
        s_found = sem("p2_dinv_candidates_ready")
        s_sel = sem("p2_dinv_selected")
        s_meta = sem("p2_kept_meta_ready")
        s_copied = sem("p2_sums_copied")
        s_turned = sem("p2_sums_turned")
        s_gathered = sems("p2_rows_gathered", SLOTS)
        s_t2 = sems("n1_table_stored", TURNS)
        s_yb = sem("n1_bias_added")
        s_nm = sem("n2_minus_mean_ready")
        s_c2 = sem("n2_products")
        s_v2 = sem("n2_vector_chain")
        s_zd = sem("n2_z_ready")
        s_out = sem("s_out_stored")

        block = ctx.enter_context(nc.Block())

        def load_rounds(eng):
            return eng.snap(eng.value_load(rounds_i[0:1, 0:1], min_val=1, max_val=MAX_ROUNDS) * NB)

        def wait_table2(eng):
            for k in range(min(TURNS, NBLK)):
                eng.wait_ge(s_t2[k], 16 * ((NBLK - k + TURNS - 1) // TURNS))

        def sum_psum(s):
            return psum[:, s, 0:WIN], psum[0:1, s, WIN:2 * WIN]

        def candidates(q, u):
            return psum[:, 4 + q, u * NT:(u + 1) * NT]

        assert KEPT * NT <= 512

        def degrees(sp, p, row, n):
            sp.wait_ge(p.done, 1)
            sp.dma_start(deg_lin[n:n + 1, :], row[:, 0:NPAD]).then_inc(s_dg, 16)
            sp.wait_ge(s_dg, 16 * (n + 1))
            sp.dma_start(deg_t[0:NT, :], deg_lin[n, :].rearrange("(t p) -> t p", p=P)).then_inc(s_dgl, 16)

        @block.sync
        def _(sp):
            sp.wait_ge(s_pads, 1)
            for raw, ind, done in ((raw_dst, dst, s_dst), (raw_src, src, s_src)):
                for c in range(CH):
                    lo, hi = c * P, min(FULL, (c + 1) * P)
                    if hi > lo:
                        sp.dma_start(raw[0:hi - lo, c, :],
                                     ind[lo * BATCH:hi * BATCH].rearrange("(g e) -> g e", e=BATCH)).then_inc(done, 16)
                if REST:
                    sp.dma_start(raw[FULL % P:FULL % P + 1, FULL // P, 0:REST],
                                 ind[FULL * BATCH:E].rearrange("(g e) -> g e", g=1)).then_inc(done, 16)
            for t, w in enumerate((W1, W2)):
                sp.dma_start(w_raw[:, t, :], w).then_inc(s_w, 16)
            sp.dma_start(w_ab[:, 0, :], mlp_w1[0:C, :]).then_inc(s_w, 16)
            sp.dma_start(w_ab[:, 1, :], mlp_w1[C:2 * C, :]).then_inc(s_w, 16)
            sp.dma_start(cw[:, :], conv_w).then_inc(s_w, 16)
            sp.wait_ge(s_cst, 1)
            sp.dma_start(bias[0:1, 0, :], b1.rearrange("(a n) -> a n", a=1)).then_inc(s_w, 16)
            sp.dma_start(bias[0:1, 1, H:2 * H], mlp_b1.rearrange("(a n) -> a n", a=1)).then_inc(s_w, 16)
            sp.dma_start(bias[0:1, 2, :], conv_b.rearrange("(a n) -> a n", a=1)).then_inc(s_w, 16)
            sp.dma_start(w2_row[0:1, 0:H], mlp_w2.rearrange("h a -> a h")).then_inc(s_w, 16)
            sp.dma_start(w2_row[0:1, H:H + 1], mlp_b2.rearrange("(a n) -> a n", a=1)).then_inc(s_w, 16)
            sp.dma_start(x_pad[0:N, :], x).then_inc(s_xpad, 16)
            for lo in range(N, XPAD, P):
                m = min(P, XPAD - lo)
                sp.dma_start(x_pad[lo:lo + m, :], zeros[0:m, :]).then_inc(s_xpad, 16)
            sp.dma_start(dst_part[NPAD:COLS, :], zeros[0:WIN, 0:H]).then_inc(s_zero, 16)
            sp.wait_ge(s_win, 1)
            end = load_rounds(sp)

            def load_idx(p, c, b, s, first=0):
                sp.wait_ge(p.used, c * SLOTS + (s + 1))
                at = b * (SLOTS * UNITS) + (s * UNITS + first)
                sp.dma_start(idx[:, s, first:UNITS], src_all[:, bass.ds(at, UNITS - first)]).then_inc(p.idx_full[s], 16)

            sp.wait_ge(s_xpad, 16 * (1 + -(-(XPAD - N) // P)))
            with sp.Fori(0, end, NB) as c0:
                with sp.Fori(0, NB) as b:
                    c = c0 + b
                    for s in range(SLOTS):
                        load_idx(p0, c, b, s)
                    sp.wait_ge(s_tt, c + 1)
                    sp.dma_start(x_tile, x_pad[bass.ds(b * P, P), :]).then_inc(s_tile, 16)
            degrees(sp, p0, deg0_row, 0)
            for b in range(NBLK):
                sp.wait_ge(s_ta, b + 1)
                sp.dma_start(table1[b * BLK:(b + 1) * BLK, :].rearrange("(t p) c -> p t c", p=P), t1_blk(b)).then_inc(s_ts[b % 2], 16)
                sp.wait_ge(s_td, b + 1)
                sp.dma_start(dst_part[b * BLK:(b + 1) * BLK, :].rearrange("(t p) c -> p t c", p=P), d_blk(b)).then_inc(s_tds[b % 2], 16)
            for q in range(2):
                sp.wait_ge(s_tds[q], 16 * ((NBLK + 1 - q) // 2))
            sp.wait_ge(s_zero, 16)
            with sp.Fori(0, end, NB) as c0:
                sp.wait_ge(s_win, end + c0 + 1)
                sp.sem_inc(s_gate)
                with sp.Fori(0, NB) as b:
                    c = c0 + b
                    for s in range(SLOTS):
                        load_idx(p1, c, b, s)
                        w = sp.value_load(win_cur[0:1, bass.ds(b * SLOTS + s, 1)], min_val=0, max_val=NPAD)
                        sp.dma_start(d_win[:, s, :], dst_part[bass.ds(w, WIN), :]).then_inc(s_dwin[s], 16)
            degrees(sp, p1, deg1_row, 1)
            for b in range(NBLK):
                sp.wait_ge(s_s2, b + 1)
                sp.dma_start(table2[b * BLK:(b + 1) * BLK, :].rearrange("(t p) c -> p t c", p=P), dy_blk(b))\
                    .then_inc(s_t2[b % TURNS], 16)
            wait_table2(sp)
            sp.wait_ge(s_los, 16 * (CH + 1))
            sp.wait_ge(s_parts, 1)

            def load_lows(row, s):
                sp.dma_start(lo_rows[:, s, :], src_lo[row, :].partition_broadcast(P)).then_inc(s_lof[s], 16)

            sp.wait_ge(s_s2c, NBLK)
            for j in range(AHEAD):
                load_lows(bass.ds(j, 1), j)
            with sp.Fori(0, end, NB) as c0:
                with sp.Fori(0, NB) as b:
                    c = c0 + b
                    for s in range(SLOTS):
                        load_idx(p2, c, b, s, KEPT)
                        sp.dma_start(rows2[:, s, 0:KEPT, :].rearrange("p u c -> p (u c)"),
                                     edge_rows[bass.ds(b * SLOTS + s, 1), :, :].rearrange("a p n -> p (a n)"))\
                            .then_inc(p2.rows_full[s], 16)
                        sp.wait_ge(s_look, c * SLOTS + (s + AHEAD + 1))
                        load_lows(bass.ds(b * SLOTS + (s + AHEAD), 1), (s + AHEAD) % SLOTS)
            stores = 0
            for b in range(NBLK):
                sp.wait_ge(s_zd, b + 1)
                tiles = min(BT, max(0, (N - b * BLK) // P))
                lo = b * BLK
                if tiles:
                    sp.dma_start(out[lo:lo + tiles * P, :].rearrange("(t p) c -> p t c", p=P),
                                 y_all[:, lo:lo + tiles * P].rearrange("p (t c) -> p t c", c=C)).then_inc(s_out, 16)
                    stores += 1
                left = min(N - lo - tiles * P, P) if tiles < BT else 0
                if left > 0:
                    sp.dma_start(out[lo + tiles * P:lo + tiles * P + left, :],
                                 y_all[0:left, lo + tiles * P:lo + (tiles + 1) * P]).then_inc(s_out, 16)
                    stores += 1
            sp.wait_ge(s_out, 16 * stores)

        @block.gpsimd
        def _(pool):
            pool.iota(lane_i[:, :], pattern=[[0, 1]], base=0, channel_multiplier=1)
            pool.iota(tile_i[:, :], pattern=[[1, NT]], base=0, channel_multiplier=0)
            pool.iota(iota_i[:, :], pattern=[[1, WIN]], base=0, channel_multiplier=0).then_inc(s_iota, 1)
            pool.memset(ident[:, :], 0.0).then_inc(s_iota, 1)
            pool.wait_ge(s_iota, 2)
            pool.affine_select(out=ident[:, :], in_=ident[:, :], compare_op=ALU.not_equal, fill=1.0, base=0,
                               pattern=[[-1, P]], channel_multiplier=1).then_inc(s_iota, 1)
            pool.wait_ge(s_win, 1)
            end = load_rounds(pool)

            def gather(p, table, place, done, first=0):
                with pool.Fori(0, end) as c:
                    for s in range(SLOTS):
                        pool.wait_ge(p.idx_full[s], (c + 1) * 16)
                        pool.sem_inc(s_gate)
                        for u in range(first, UNITS):
                            pool.indirect_dma_start(
                                out=place[:, s, u, :], out_offset=None, in_=table,
                                in_offset=bass.IndirectOffsetOnAxis(idx[:, s, u:u + 1], 0)).then_inc(done[s], 16)

            gather(p0, x, rows[:, :, :, 0:C], p0.rows_full)

            def load_x(b):
                for place, table in ((x_blk(b), x_pad), (u_blk(b), x_part)):
                    pool.dma_start(place, table[b * BLK:(b + 1) * BLK, :].rearrange("(t p) c -> p t c", p=P))\
                        .then_inc(s_xb[b % 2], 16)

            def inverse_deviations(made):
                for b in range(NBLK):
                    if made == 0 and b + 2 < NBLK:
                        pool.wait_ge(s_prep, b + 1)
                        load_x(b + 2)
                    pool.wait_ge(s_var, made + b + 1)
                    nc.gpsimd.tensor_tensor(rstd[:, b % STATS, :], rstd[:, b % STATS, :], minus_half[:, 0:BT], ALU.pow).then_inc(s_rstd, 1)

            pool.wait_ge(s_tst, end * 16)
            pool.sem_inc(s_gate)
            load_x(0)
            load_x(1)
            inverse_deviations(0)
            for q in range(2):
                pool.wait_ge(s_ts[q], 16 * ((NBLK + 1 - q) // 2))
            gather(p1, table1, rows, p1.rows_full)
            pool.wait_ge(s_dgn, 2)
            for b in range(NBLK):
                part = degn[:, b * BT:(b + 1) * BT]
                nc.gpsimd.tensor_tensor(part, part, minus_half[:, 0:BT], ALU.pow).then_inc(s_rstd, 1)
            wait_table2(pool)
            gather(p2, table2, rows2, s_gathered, KEPT)
            inverse_deviations(NBLK)

        @block.tensor
        def _(pe):
            pe.wait_ge(s_iota, 3)
            pe.wait_ge(s_cst, 1)
            n = 0
            for a in range(2):
                for c in range(CH):
                    pe.wait_ge(s_float, a * CH + c + 1)
                    for h in range(UNITS // 4):
                        if n >= 4:
                            pe.wait_ge(s_ev, n - 3)
                        for u in range(4):
                            q = 4 * h + u
                            last = nc.tensor.transpose(psum[:, n % 4, u * P:(u + 1) * P],
                                                       raw_f[:, c, q * P:(q + 1) * P], ident[:, :])
                        last.then_inc(s_tr, 1)
                        n += 1
            pe.wait_ge(s_pv, 1)
            for c in range(CH):
                m = min(P, NG - c * P)
                nc.tensor.transpose(psum[0:m, 4, c * P:(c + 1) * P], gmin[:, c * P:c * P + m], ident[:, :])
                last = nc.tensor.transpose(psum[0:m, 5, c * P:(c + 1) * P], gmax[:, c * P:c * P + m], ident[:, :])
            last.then_inc(s_pp, 1)
            pe.wait_ge(s_pv, 2)
            for c in range(CH):
                m = min(P, NG - c * P)
                nc.tensor.matmul(psum[:, 6, c * P:c * P + m], ones[0:m, :], raw_f[0:m, 0, c * P:c * P + m],
                                 start=True, stop=True)
            nc.tensor.transpose(psum[0:1, 7, 0:P], span1[:, :], ident[:, :]).then_inc(s_pp, 1)
            pe.wait_ge(s_pv, 3)
            nc.tensor.transpose(psum[:, 0, 0:P], w_diff[:, :], ident[:, :])
            nc.tensor.transpose(psum[:, 0, P:2 * P], w_raw[:, 1, :], ident[:, :])
            nc.tensor.matmul(psum[:, 0, 2 * P:2 * P + H + 1], ones[:, :], w2_row[:, :], start=True, stop=True)
            nc.tensor.matmul(psum[:, 1, 0:2 * C], ones[:, :], bias[:, 1:3, :].rearrange("p a c -> p (a c)"),
                             start=True, stop=True).then_inc(s_pp, 1)

            def load_end():
                pe.wait_ge(s_win, 1)
                return load_rounds(pe)

            end = load_end()
            pe.sem_inc(p0.used, SLOTS)
            pe.sem_inc(s_tt, 1)

            def turn_x(c):
                pe.wait_ge(s_tile, (c + 1) * 16)
                pe.sem_inc(s_gate)
                nc.tensor.transpose(psum[:, 4, 0:P], x_tile, ident[:, :]).then_inc(s_tt, 1)

            def x_product(c):
                pe.wait_ge(s_tc, c + 1)
                pe.wait_ge(s_to, c + 1)
                nc.tensor.matmul(psum[:, 5, 0:C], xt_tile, wd_t[:, :], start=True, stop=False)
                nc.tensor.matmul(psum[:, 5, 0:C], ones[:, :], bias[:, 0, :], start=False, stop=True).then_inc(s_tu, 1)

            def sums(p, c, s, deg):
                pe.wait_ge(p.rows_full[s], (c + 1) * (16 * UNITS))
                pe.wait_ge(p.onehot, c * SLOTS + (s + 1))
                pe.wait_ge(p.added, c * SLOTS + (s + 1))
                total, count = sum_psum(s)
                for u in range(UNITS):
                    last = nc.tensor.matmul(total, rows[:, s, u, 0:C], onehot[:, s, u, :],
                                            start=(u == 0), stop=(u == UNITS - 1))
                if deg:
                    for u in range(UNITS):
                        last = nc.tensor.matmul(count, ones[:, 0:1], onehot[:, s, u, :],
                                                start=(u == 0), stop=(u == UNITS - 1))
                last.then_inc(p.used, 1)

            with pe.Fori(0, end) as c:
                for s in range(SLOTS):
                    sums(p0, c, s, True)
                    if s == 0:
                        turn_x(c)
                    if s == 1:
                        x_product(c)

            def degree_tile(n):
                pe.wait_ge(s_dgl, 16 * (n + 1))
                nc.tensor.transpose(psum[:, 7, 0:NT], deg_t[0:NT, :], ident[0:NT, 0:NT]).then_inc(s_dgt, 1)

            degree_tile(0)

            def sum_products(b):
                if b >= 2:
                    pe.wait_ge(s_used0, b - 1)
                for t in range(BT):
                    o = (1 + b % 2) * 1024 + t * P
                    last = nc.tensor.matmul(ps_flat[:, o:o + P], acc[:, b * BLK + t * P:b * BLK + (t + 1) * P],
                                            w2_t[:, :], start=True, stop=True)
                last.then_inc(s_uv, 1)

            def turn_y(b):
                pe.wait_ge(s_y0, b + 1)
                if b:
                    pe.wait_ge(s_yc, b)
                for t in range(BT):
                    o = b * BLK + t * P
                    last = nc.tensor.transpose(ps_flat[:, t * P:(t + 1) * P], y_all[:, o:o + P], ident[:, :])
                last.then_inc(s_yt, 1)

            def table_products(b):
                pe.wait_ge(s_yc, b + 1)
                if b:
                    pe.wait_ge(s_ta, b)
                    pe.wait_ge(s_td, b)
                for t in range(BT):
                    last = nc.tensor.matmul(ps_flat[:, 3072 + t * P:3072 + (t + 1) * P], yt_blk[:, t * P:(t + 1) * P],
                                            w_ab[:, :, :].rearrange("p a h -> p (a h)"), start=True, stop=True)
                last.then_inc(s_ab, 1)

            pe.wait_ge(s_to, end + 1)
            pe.sem_inc(s_gate)
            sum_products(0)
            sum_products(1)
            for b in range(NBLK):
                if b + 2 < NBLK:
                    sum_products(b + 2)
                turn_y(b)
                table_products(b)
            pe.sem_inc(p1.used, SLOTS)

            def oh_psum(b):
                return ps_flat[0:WIN, b * 1024:(b + 1) * 1024]

            def turn(c, s):
                at = (s + AHEAD) % SLOTS
                pe.wait_ge(p1.onehot, c * SLOTS + (s + AHEAD + 1))
                pe.wait_ge(s_ohc, c * SLOTS + (s + AHEAD + 1))
                pe.sem_inc(s_gate)
                for u in range(UNITS):
                    last = nc.tensor.transpose(oh_psum(at % 2)[:, u * P:(u + 1) * P], onehot[:, at, u, :], ident[:, :])
                last.then_inc(s_oht, 1)

            def dst_rows(c, s):
                pe.wait_ge(s_dwin[s], (c + 1) * 16)
                pe.wait_ge(s_ohc, c * SLOTS + (s + 3))
                pe.wait_ge(s_zc, c * SLOTS + (s + 1))
                for u in range(UNITS):
                    last = nc.tensor.matmul(psum[:, 4 + s % 2, u * H:(u + 1) * H], oh_t[:, s % 2, u, :],
                                            d_win[:, s, :], start=True, stop=True)
                last.then_inc(s_z, 1)

            def degree_sum(c, s):
                pe.wait_ge(s_ew, c * SLOTS + (s + 1))
                pe.wait_ge(p1.added, c * SLOTS + (s + 1))
                pe.wait_ge(s_rs[s], (c + 1) * 16)
                for u in range(UNITS):
                    last = nc.tensor.matmul(psum[0:1, 6 + s % 2, 0:WIN], ew[:, s, u:u + 1], onehot[:, s, u, :],
                                            start=(u == 0), stop=(u == UNITS - 1))
                last.then_inc(p1.used, 1)

            for j in range(AHEAD):
                turn(0, j - AHEAD)
            with pe.Fori(0, end) as c:
                dst_rows(c, 0)
                for s in range(SLOTS):
                    if s + 1 < SLOTS:
                        dst_rows(c, s + 1)
                    turn(c, s)
                    degree_sum(c, s)

            degree_tile(1)
            pe.wait_ge(s_ohc, end * SLOTS + 3)
            pe.sem_inc(s_gate)
            for b in range(NBLK):
                pe.wait_ge(s_s2, b + 1)
                if b >= 2:
                    pe.wait_ge(s_s2c, b - 1)
                for t in range(BT):
                    o = (b % 2) * 1024 + t * P
                    last = nc.tensor.transpose(ps_flat[:, o:o + P], dy_blk(b)[:, t, :], ident[:, :])
                last.then_inc(s_s2t, 1)
            pe.sem_inc(p2.used, SLOTS)
            pe.wait_ge(s_s2c, NBLK)
            pe.wait_ge(s_parts, 1)

            def look_up(c, s):
                q = (s + AHEAD) % 2
                pe.wait_ge(s_look, c * SLOTS + (s + AHEAD + 1 + SLOTS))
                pe.wait_ge(s_sel, c * SLOTS + (s + AHEAD + 1))
                for u in range(KEPT):
                    for k in range(3):
                        last = nc.tensor.matmul(candidates(q, u), lo_hot[:, q, u * P:(u + 1) * P],
                                                dinv_parts[:, k, :], start=(k == 0), stop=(k == 2))
                last.then_inc(s_found, 1)

            def weighted_sums(c, s):
                pe.wait_ge(p2.rows_full[s], (c + 1) * 16)
                pe.wait_ge(s_gathered[s], (c + 1) * (16 * (UNITS - KEPT)))
                pe.wait_ge(p2.onehot, c * SLOTS + (s + 1))
                pe.wait_ge(s_copied, c * SLOTS + (s + 1))
                for u in range(UNITS):
                    last = nc.tensor.matmul(psum[0:WIN, s, 0:C], onehot[:, s, u, :], rows2[:, s, u, :],
                                            start=(u == 0), stop=(u == UNITS - 1))
                last.then_inc(p2.used, 1)

            def turn_sums(c, s):
                pe.wait_ge(s_copied, c * SLOTS + (s + 1 + SLOTS))
                pe.wait_ge(p2.added, c * SLOTS + (s + 3))
                pe.sem_inc(s_gate)
                nc.tensor.transpose(psum[:, 6 + s % 2, 0:WIN], sums_sb[:, s % 2, :], ident[0:WIN, 0:WIN])\
                    .then_inc(s_turned, 1)

            pe.sem_inc(s_turned, 2)
            for j in range(AHEAD):
                look_up(0, j - AHEAD)
            with pe.Fori(0, end) as c:
                for s in range(SLOTS):
                    weighted_sums(c, s)
                    look_up(c, s)
                    turn_sums(c, s)

            for b in range(NBLK):
                if b == 0:
                    pe.wait_ge(p2.done, 1)
                if b >= 4:
                    pe.wait_ge(s_v2, CHAIN2 * (b - 4) + 1)
                for t in range(BT):
                    o = (b % 4) * 1024 + t * P
                    last = nc.tensor.matmul(ps_flat[:, o:o + P], acc[:, b * BLK + t * P:b * BLK + (t + 1) * P],
                                            cw[:, :], start=True, stop=True)
                last.then_inc(s_c2, 1)

        @block.scalar
        def _(act):
            act.wait_ge(s_win, 1)
            end = load_rounds(act)
            nc.scalar.activation(acc[:, :], zeros[:, 0:1].to_broadcast([P, COLS]), ACT.Copy).then_inc(s_clear, 1)
            act.wait_ge(s_lo, 1)
            for c in range(CH):
                m = min(P, NG - c * P)
                act.dma_start(src_lo[c * P:c * P + m, :], lo_all[0:m, c, 0:KEPT_EDGES]).then_inc(s_los, 16)
            act.dma_start(src_lo[NG:NG + AHEAD, :], lo_all[0:AHEAD, 0, 0:KEPT_EDGES]).then_inc(s_los, 16)

            nc.scalar.activation(deg0_row, zeros[0:1, 0:1].to_broadcast([1, COLS]), ACT.Copy).then_inc(s_clear, 1)
            act.sem_inc(s_to, 1)
            with act.Fori(0, end, NB) as c0, act.Fori(0, NB) as b:
                c = c0 + b
                act.wait_ge(s_tt, c + 2)
                nc.scalar.activation(xt_tile, psum[:, 4, 0:P], ACT.Copy).then_inc(s_tc, 1)
                act.wait_ge(s_tu, c + 1)
                nc.scalar.activation(u_tile, psum[:, 5, 0:C], ACT.Copy).then_inc(s_to, 1)
                act.wait_ge(s_to, c + 2)
                act.dma_start(x_part[bass.ds(b * P, P), :], u_tile).then_inc(s_tst, 16)
                act.wait_ge(s_tst, (c + 1) * 16)
                act.sem_inc(s_gate)

            def normalise(b, v, ready, done):
                act.wait_ge(ready, b + 1)
                q = b % STATS
                for t in range(BT):
                    last = nc.scalar.activation(
                        y_all[:, b * BLK + t * P:b * BLK + (t + 1) * P], v[:, t, :], ACT.Identity,
                        bias=minus_mean[:, q, t:t + 1], scale=rstd[:, q, t:t + 1])
                last.then_inc(done, 1)

            def copy_ya(b):
                act.wait_ge(s_ab, b + 1)
                ab = ps_flat[:, 3072:3072 + BLK].rearrange("p (t c) -> p t c", c=C)
                nc.scalar.activation(t1_blk(b)[:, :, 0:H], ab[:, :, 0:H], ACT.Copy).then_inc(s_ta, 1)

            for b in range(NBLK):
                normalise(b, v_blk(b), s_nm0, s_y0)
                if b:
                    copy_ya(b - 1)
                if b >= 2:
                    act.wait_ge(s_ts[b % 2], 16 * (b // 2))
                act.wait_ge(s_y0, b + 1)
                nc.scalar.activation(t1_blk(b)[:, :, H:ROW], blk(y_all[:, b * BLK:(b + 1) * BLK]), ACT.Copy)
                act.wait_ge(s_yt, b + 1)
                nc.scalar.activation(yt_blk, ps_flat[:, 0:BLK], ACT.Copy).then_inc(s_yc, 1)
            copy_ya(NBLK - 1)

            act.sem_inc(s_ohc, 2)
            act.wait_ge(s_oht, 1)
            act.wait_ge(s_zc, 2)
            nc.scalar.activation(oh_t[:, 0, :, :].rearrange("w u p -> w (u p)"), ps_flat[0:WIN, 0:1024],
                                 ACT.Copy).then_inc(s_ohc, 1)
            with act.Fori(0, end, NB) as c0, act.Fori(0, NB) as b:
                c = c0 + b

                def copy_turned(s):
                    act.wait_ge(s_oht, c * SLOTS + (s + 1))
                    act.wait_ge(s_zc, c * SLOTS + (s + 1))
                    nc.scalar.activation(oh_t[:, s % 2, :, :].rearrange("w u p -> w (u p)"),
                                         ps_flat[0:WIN, (s % 2) * 1024:(s % 2 + 1) * 1024], ACT.Copy).then_inc(s_ohc, 1)

                def weigh(s):
                    act.wait_ge(s_zc, c * SLOTS + (s + 3))
                    nc.scalar.activation(gelu_edge[:, s % 2, :, :], z_edge[:, s, :, :], ACT.Gelu)\
                        .then_inc(s_gelu, 1)
                    act.dma_start(edge_rows[bass.ds(b * SLOTS + s, 1), :, :].rearrange("a p (u c) -> p (a u) c", c=C),
                                  rows[:, s, 0:KEPT, H:ROW]).then_inc(s_rs[s], 16)
                    act.wait_ge(s_log, c * SLOTS + (s + 1))
                    nc.scalar.activation(tanh_edge[:, s, :], logit[:, s, :], ACT.Tanh, scale=0.5,
                                         bias=w2_all[:, H:H + 1]).then_inc(s_tanh, 1)

                for s in range(SLOTS):
                    copy_turned(s + 1)
                    weigh(s)
            for b in range(NBLK):
                act.wait_ge(s_s2t, b + 1)
                o = (b % 2) * 1024
                nc.scalar.activation(acc[:, b * BLK:(b + 1) * BLK], ps_flat[:, o:o + BLK], ACT.Copy).then_inc(s_s2c, 1)
            act.wait_ge(s_parts, 1)
            act.sem_inc(s_copied, SLOTS)

            def copy_meta(at, m):
                nc.scalar.activation(weight[:, m % SLOTS, KEPT:UNITS], meta[:, 1, bass.ds(at + KEPT, UNITS - KEPT)], ACT.Copy)
                nc.scalar.activation(kept_meta[:, m % SLOTS, :, :], meta[:, 1:3, bass.ds(at, KEPT)],
                                     ACT.Copy).then_inc(s_meta, 1)

            copy_meta(0, 0)
            with act.Fori(0, end, NB) as c0, act.Fori(0, NB) as b:
                c = c0 + b
                for s in range(SLOTS):
                    act.wait_ge(p2.added, c * SLOTS + (s + 2))
                    copy_meta(b * (SLOTS * UNITS) + (s + 1) * UNITS, s + 1)
                    act.wait_ge(p2.used, c * SLOTS + (s + 1 + SLOTS))
                    act.wait_ge(s_turned, c * SLOTS + (s + 1))
                    nc.scalar.activation(sums_sb[:, s % 2, :], psum[0:WIN, s, 0:C], ACT.Copy).then_inc(s_copied, 1)

            for b in range(NBLK):
                normalise(b, dy_blk(b), s_nm, s_zd)

        @block.vector
        def _(dve):
            made = [0]

            def chain(ins, s=s_chain):
                made[0] += 1
                ins.then_inc(s, 1)
                dve.wait_ge(s, made[0])

            for c in range(FULL // P, CH):
                nc.vector.memset(raw_src[:, c, :], 0)
                nc.vector.memset(raw_dst[:, c, :], PAD_DST)
            nc.vector.memset(zeros[:, :], 0.0).then_inc(s_pads, 1)
            nc.vector.memset(ones[:, :], 1.0)
            nc.vector.memset(span_t[:, :], 0.0)
            nc.vector.memset(minus_half[:, :], -0.5)
            nc.vector.memset(w2_row[:, :], 0.0)
            nc.vector.memset(bias[:, :, :], 0.0).then_inc(s_cst, 1)
            loads = sum(1 for c in range(CH) if min(FULL, (c + 1) * P) > c * P) + (REST > 0)
            n = 0
            for a, (raw, done, to) in enumerate(((raw_dst, s_dst, dst_rel), (raw_src, s_src, src_all))):
                dve.wait_ge(done, 16 * loads)
                if a:
                    dve.wait_ge(s_tr, n)
                for c in range(CH):
                    nc.vector.tensor_copy(raw_f[:, c, :], raw[:, c, :]).then_inc(s_float, 1)
                for c in range(CH):
                    m = min(P, NG - c * P)
                    for h in range(UNITS // 4):
                        dve.wait_ge(s_tr, n + 1)
                        nc.vector.tensor_copy(
                            to.rearrange("p (g u) -> p u g", u=UNITS)[:, 4 * h:4 * h + 4, c * P:c * P + m],
                            psum[:, n % 4, :].rearrange("p (u g) -> p u g", u=4)[:, :, 0:m]).then_inc(s_ev, 1)
                        n += 1
                if a == 0:
                    dve.wait_ge(s_ev, n)
                    chain(nc.vector.tensor_scalar(capped, dst_rel, float(N - 1), None, ALU.min))
                    nc.vector.tensor_reduce(gmin, dst_rel.rearrange("p (g u) -> p g u", u=UNITS), AX, ALU.min)
                    nc.vector.tensor_reduce(gmax, capped.rearrange("p (g u) -> p g u", u=UNITS), AX, ALU.max)\
                        .then_inc(s_pv, 1)
            dve.wait_ge(s_pp, 1)
            for c in range(CH):
                m = min(P, NG - c * P)
                nc.vector.tensor_reduce(gmin_t[0:m, c:c + 1], psum[0:m, 4, c * P:(c + 1) * P], AX, ALU.min)
                chain(nc.vector.tensor_reduce(span_t[0:m, c:c + 1], psum[0:m, 5, c * P:(c + 1) * P], AX, ALU.max))
                nc.vector.tensor_tensor(span_t[0:m, c:c + 1], span_t[0:m, c:c + 1], gmin_t[0:m, c:c + 1], ALU.subtract)
                chain(nc.vector.tensor_scalar(raw_f[0:m, 0, c * P:c * P + m], ident[0:m, 0:m],
                                              gmin_t[0:m, c:c + 1], None, ALU.mult))
            nc.vector.tensor_reduce(span1[:, :], span_t[:, :], AX, ALU.max).then_inc(s_pv, 1)
            dve.wait_ge(s_pp, 2)
            chain(nc.vector.tensor_scalar(base_f, psum[:, 6, 0:NG], float(NPAD), None, ALU.min))
            nc.vector.tensor_copy(win_base[0:1, :], base_f[0:1, :])
            nc.vector.tensor_copy(win_cur[0:1, :], base_f[0:1, :])
            chain(nc.vector.tensor_reduce(span1[0:1, :], psum[0:1, 7, 0:P], AX, ALU.max))
            chain(nc.vector.tensor_scalar(span1[0:1, :], span1[0:1, :], float(2 * STEP - WIN), float(STEP), ALU.add, ALU.max))
            chain(nc.vector.tensor_copy(rounds_i[0:1, 1:2], span1[0:1, :]))
            chain(nc.vector.tensor_scalar(rounds_i[0:1, 0:1], rounds_i[0:1, 1:2], STEP.bit_length() - 1, None,
                                          ALU.logical_shift_right))
            dve.wait_ge(s_iota, 1)
            nc.vector.tensor_copy(iota0[:, :], iota_i[:, :])
            nc.vector.tensor_copy(iota_cur[:, :], iota_i[:, :])
            nc.vector.tensor_copy(lane[:, :], lane_i[:, :])
            nc.vector.tensor_copy(tile_no[:, :], tile_i[:, :]).then_inc(s_win, 1)
            chain(nc.vector.tensor_tensor(dst_rel.rearrange("p (g u) -> p g u", u=UNITS),
                                          dst_rel.rearrange("p (g u) -> p g u", u=UNITS),
                                          base_f.unsqueeze(2).to_broadcast([P, NG, UNITS]), ALU.subtract))
            nc.vector.tensor_scalar(meta_next_round[:, 0, :], dst_rel[:, 0:AHEAD * UNITS], float(WIN), None, ALU.subtract)
            chain(nc.vector.tensor_scalar(raw_src, raw_src, P - 1, None, ALU.bitwise_and))
            nc.vector.tensor_copy(lo_all, raw_src).then_inc(s_lo, 1)
            dve.wait_ge(s_w, 160)
            nc.vector.tensor_tensor(w_diff[:, :], w_raw[:, 0, :], w_raw[:, 1, :], ALU.subtract).then_inc(s_pv, 1)
            dve.wait_ge(s_pp, 3)
            nc.vector.tensor_copy(wd_t[:, :], psum[:, 0, 0:P])
            nc.vector.tensor_copy(w2_t[:, :], psum[:, 0, P:2 * P])
            nc.vector.tensor_scalar(w2_all[:, H:H + 1], psum[:, 0, 2 * P + H:2 * P + H + 1], 0.5, None, ALU.mult)
            nc.vector.tensor_copy(dst_bias[:, :], psum[:, 1, H:2 * H])
            nc.vector.tensor_copy(conv_bias[:, :], psum[:, 1, C:2 * C])
            nc.vector.tensor_copy(w2_all[:, 0:H], psum[:, 0, 2 * P:2 * P + H]).then_inc(p0.added, SLOTS)

            end = load_rounds(dve)

            def dst_cols(b, s):
                return bass.ds(b * (SLOTS * UNITS) + s * UNITS, UNITS)

            def window(b, s):
                return dve.value_load(win_cur[0:1, bass.ds(b * SLOTS + s, 1)], min_val=0, max_val=NPAD)

            def make_onehot(b, s):
                return nc.vector.tensor_tensor(
                    onehot[:, s % SLOTS, :, :],
                    meta[:, 0, dst_cols(b, s)].unsqueeze(2).to_broadcast([P, UNITS, WIN]),
                    iota_cur[:, :].unsqueeze(1).to_broadcast([P, UNITS, WIN]), ALU.is_equal)

            def next_round():
                nc.vector.tensor_scalar(iota_cur[:, :], iota_cur[:, :], float(WIN), None, ALU.add)
                nc.vector.tensor_scalar(win_cur[:, :], win_cur[:, :], float(WIN), float(NPAD), ALU.add, ALU.min)\
                    .then_inc(s_win, NB)

            def end_pass(p, n):
                dve.wait_ge(s_win, end * (n + 1) + 1)
                nc.vector.tensor_copy(iota_cur[:, :], iota0[:, :])
                nc.vector.tensor_copy(win_cur[:, :], win_base[:, :]).then_inc(p.done, 1)
                dve.wait_ge(p.done, 1)

            dve.wait_ge(s_clear, 2)
            with dve.Fori(0, end, NB) as c0:
                dve.wait_ge(s_win, c0 + 1)
                dve.sem_inc(s_gate)
                with dve.Fori(0, NB) as b:
                    c = c0 + b
                    for s in range(SLOTS):
                        make_onehot(b, s).then_inc(p0.onehot, 1)
                    for s in range(SLOTS):
                        w = window(b, s)
                        dve.wait_ge(p0.used, c * SLOTS + (s + 1 + SLOTS))
                        dve.wait_ge(p0.added, c * SLOTS + (s + SLOTS))
                        total, count = sum_psum(s)
                        nc.vector.tensor_tensor(acc[:, bass.ds(w, WIN)], acc[:, bass.ds(w, WIN)], total, ALU.add)
                        nc.vector.tensor_tensor(deg0_row[:, bass.ds(w, WIN)], deg0_row[:, bass.ds(w, WIN)], count,
                                                ALU.add).then_inc(p0.added, 1)
                next_round()
            end_pass(p0, 0)

            def degree_tile(n):
                dve.wait_ge(s_dgt, n + 1)
                return nc.vector.tensor_copy(degn[:, :], psum[:, 7, 0:NT])

            degree_tile(0).then_inc(s_dgn, 1)
            dve.wait_ge(s_dgn, 1)

            n0 = [0]

            def link0(ins):
                n0[0] += 1
                ins.then_inc(s_v0, 1)
                dve.wait_ge(s_v0, n0[0])

            def by_node(b):
                return degn[:, b * BT:(b + 1) * BT].unsqueeze(2).to_broadcast([P, BT, C])

            def x_terms(b):
                dve.wait_ge(s_xb[b % 2], 32 * (b // 2 + 1))
                if b >= 2:
                    dve.wait_ge(s_y0, b - 1)
                link0(nc.vector.tensor_tensor(v_blk(b), u_blk(b), by_node(b), ALU.mult))
                nc.vector.tensor_tensor(v_blk(b), v_blk(b), x_blk(b), ALU.add).then_inc(s_prep, 1)

            def residual0(b):
                v, q = v_blk(b), b % STATS
                dve.wait_ge(s_prep, b + 1)
                dve.wait_ge(s_uv, b + 1)
                o = (1 + b % 2) * 1024
                nc.vector.tensor_tensor(v, v, blk(ps_flat[:, o:o + BLK]), ALU.add).then_inc(s_used0, 1)
                dve.wait_ge(s_used0, b + 1)
                normal_statistics(v, q, link0)

            def normal_statistics(v, q, link):
                for t in range(BT):
                    last = nc.vector.bn_stats(bn[:, q, t, :], v[:, t, :])
                link(last)
                for t in range(BT):
                    last = nc.vector.bn_aggr(mv[:, q, t, :], bn[:, q, t, :])
                link(last)
                nc.vector.tensor_scalar(rstd[:, q, :], mv[:, q, :, 1:2].rearrange("p t a -> p (t a)"), EPS, None,
                                        ALU.add).then_inc(s_var, 1)

            def minus_means(b, made, done):
                q = b % STATS
                dve.wait_ge(s_rstd, made)
                nc.vector.scalar_tensor_tensor(minus_mean[:, q, :], mv[:, q, :, 0:1].rearrange("p t a -> p (t a)"), -1.0,
                                               rstd[:, q, :], ALU.mult, ALU.mult).then_inc(done, 1)

            def finish_dst(b):
                dve.wait_ge(s_ta, b + 1)
                if b >= 2:
                    dve.wait_ge(s_tds[b % 2], 16 * (b // 2))
                nc.vector.tensor_tensor(d_blk(b), blk(ps_flat[:, 3072:3072 + BLK])[:, :, H:2 * H],
                                        dst_bias[:, :].unsqueeze(1).to_broadcast([P, BT, H]), ALU.add).then_inc(s_td, 1)

            x_terms(0)
            residual0(0)
            for b in range(NBLK):
                if b + 1 < NBLK:
                    x_terms(b + 1)
                minus_means(b, b + 1, s_nm0)
                if b + 1 < NBLK:
                    residual0(b + 1)
                if b:
                    finish_dst(b - 1)
            finish_dst(NBLK - 1)

            dve.wait_ge(s_los, 16 * (CH + 1))
            nc.vector.memset(ew_all, 0.0)
            nc.vector.memset(deg1_row, 1.0).then_inc(p1.chain, 1)
            dve.wait_ge(p1.chain, 1)
            dve.wait_ge(s_ta, NBLK)
            dve.sem_inc(p1.added, 2)
            dve.sem_inc(s_zc, 2)
            K = 4 * SLOTS
            for j in range(AHEAD):
                make_onehot(0, j).then_inc(p1.onehot, 1)
            with dve.Fori(0, end, NB) as c0:
                dve.wait_ge(s_win, end + c0 + 1)
                dve.sem_inc(s_gate)
                with dve.Fori(0, NB) as b:
                    c = c0 + b
                    def add_degrees(s):
                        w = window(b, s)
                        dve.wait_ge(p1.used, c * SLOTS + (s + 1 + SLOTS))
                        dve.wait_ge(p1.added, c * SLOTS + (s + 2))
                        nc.vector.tensor_tensor(deg1_row[:, bass.ds(w, WIN)], deg1_row[:, bass.ds(w, WIN)],
                                                psum[0:1, 6 + s % 2, 0:WIN], ALU.add).then_inc(p1.added, 1)

                    for s in range(SLOTS):
                        def chained(ins, j):
                            ins.then_inc(p1.chain, 1)
                            dve.wait_ge(p1.chain, c * K + (4 * s + j + 1))

                        dve.wait_ge(s_z, c * SLOTS + (s + 1))
                        dve.wait_ge(p1.rows_full[s], (c + 1) * (16 * UNITS))
                        zs = z_edge[:, s, :, :]
                        nc.vector.tensor_tensor(
                            zs, psum[:, 4 + s % 2, :].rearrange("p (u h) -> p u h", h=H), rows[:, s, :, 0:H],
                            ALU.add).then_inc(s_zc, 1)
                        dve.wait_ge(p1.used, c * SLOTS + (s + AHEAD + 1))
                        make_onehot(b, s + AHEAD).then_inc(p1.onehot, 1)
                        cols = dst_rel[:, dst_cols(b, s)]
                        chained(nc.vector.tensor_scalar(mask[:, s, :], cols, iota_cur[:, 0:1], 0.5,
                                                        ALU.is_ge, ALU.mult), 1)
                        chained(nc.vector.scalar_tensor_tensor(mask[:, s, :], cols, iota_cur[:, WIN - 1:WIN],
                                                               mask[:, s, :], ALU.is_le, ALU.mult), 2)
                        dve.wait_ge(s_gelu, c * SLOTS + (s + 1))
                        chained(nc.vector.tensor_tensor(zs, gelu_edge[:, s % 2, :, :], w2_all[:, 0:H].unsqueeze(1)
                                                        .to_broadcast([P, UNITS, H]), ALU.mult), 3)
                        nc.vector.tensor_reduce(logit[:, s, :], zs, AX, ALU.add).then_inc(s_log, 1)
                        if s:
                            add_degrees(s - 1)
                        dve.wait_ge(s_tanh, c * SLOTS + (s + 1))
                        nc.vector.scalar_tensor_tensor(ew[:, s, :], tanh_edge[:, s, :], 1.0, mask[:, s, :],
                                                       ALU.add, ALU.mult).then_inc(s_ew, 1)
                        dve.wait_ge(s_ew, c * SLOTS + (s + 1))
                        at = ew_all[:, dst_cols(b, s)]
                        chained(nc.vector.tensor_tensor(at, at, ew[:, s, :], ALU.add), 4)
                    add_degrees(SLOTS - 1)
                next_round()
            end_pass(p1, 1)

            degree_tile(1).then_inc(s_dgn, 1)
            dve.wait_ge(s_dgn, 2)
            for b in range(NBLK):
                if b >= TURNS:
                    dve.wait_ge(s_s2t, b - TURNS + 1)
                    dve.wait_ge(s_t2[b % TURNS], 16 * (b // TURNS))
                dve.wait_ge(s_rstd, NBLK + b + 1)
                nc.vector.tensor_tensor(dy_blk(b), blk(y_all[:, b * BLK:(b + 1) * BLK]), by_node(b),
                                        ALU.mult).then_inc(s_s2, 1)
            rest = dinv_rest[:, :]
            for k in range(3):
                part = dinv_parts[:, k, :]
                chain(nc.vector.tensor_copy(part, degn[:, :] if k == 0 else rest))
                if k < 2:
                    chain(nc.vector.tensor_tensor(rest, degn[:, :] if k == 0 else rest, part, ALU.subtract))
            kept_src = src_all.rearrange("p (g u) -> p g u", u=UNITS)[:, :, 0:KEPT]
            kept_hi = src_hi.rearrange("p (g u) -> p g u", u=UNITS)[:, :, 0:KEPT]
            chain(nc.vector.tensor_scalar(kept_src, kept_src, P.bit_length() - 1, None, ALU.logical_shift_right))
            chain(nc.vector.tensor_copy(kept_hi, kept_src))
            nc.vector.tensor_copy(meta_next_round[:, 1:3, :], meta[:, 1:3, 0:AHEAD * UNITS]).then_inc(s_parts, 1)
            for b in range(NBLK):
                dve.wait_ge(s_s2, b + 1)
                y = blk(y_all[:, b * BLK:(b + 1) * BLK])
                nc.vector.tensor_tensor(y, y, conv_bias[:, :].unsqueeze(1).to_broadcast([P, BT, C]), ALU.add).then_inc(s_yb, 1)
            wait_table2(dve)
            dve.wait_ge(s_s2c, NBLK)
            dve.sem_inc(p2.added, SLOTS)
            dve.sem_inc(s_look, SLOTS)
            dve.sem_inc(s_sel, 2)

            def low_one_hot(c, s):
                at = (s + AHEAD) % SLOTS
                dve.wait_ge(s_lof[at], (c + (1 + (s + AHEAD) // SLOTS)) * 16)
                nc.vector.tensor_scalar(lo_hot[:, (s + AHEAD) % 2, :], lo_rows[:, at, :], lane[:, :], None,
                                        ALU.is_equal).then_inc(s_look, 1)

            def weigh(c, b, m):
                s = m % SLOTS
                make_onehot(b, m).then_inc(p2.chain, 1)
                dve.wait_ge(s_meta, c * SLOTS + (m + 1))
                dve.wait_ge(s_found, c * SLOTS + (m + 1))
                for u in range(KEPT):
                    last = nc.vector.scalar_tensor_tensor(
                        picked[:, u, :], tile_no[:, :], kept_meta[:, s, 1, u:u + 1], candidates(m % 2, u),
                        ALU.is_equal, ALU.mult, accum_out=dinv_src[:, s, u:u + 1])
                last.then_inc(s_sel, 1)
                w = window(b, m - 1) if m else None
                dve.wait_ge(s_sel, c * SLOTS + (m + 3))
                nc.vector.tensor_tensor(weight[:, s, 0:KEPT], dinv_src[:, s, :], kept_meta[:, s, 0, :], ALU.mult)\
                    .then_inc(p2.chain, 1)
                dve.wait_ge(p2.chain, c * (2 * SLOTS) + (2 * m + 2))
                nc.vector.tensor_tensor(onehot[:, s, :, :], onehot[:, s, :, :],
                                        weight[:, s, :].unsqueeze(2).to_broadcast([P, UNITS, WIN]),
                                        ALU.mult).then_inc(p2.onehot, 1)
                return w

            def add_sums(c, w, s):
                dve.wait_ge(s_turned, c * SLOTS + (s + 3))
                dve.wait_ge(p2.added, c * SLOTS + (s + SLOTS))
                nc.vector.tensor_tensor(acc[:, bass.ds(w, WIN)], acc[:, bass.ds(w, WIN)], psum[:, 6 + s % 2, 0:WIN],
                                        ALU.add).then_inc(p2.added, 1)

            for j in range(AHEAD):
                low_one_hot(0, j - AHEAD)
            weigh(0, 0, 0)
            with dve.Fori(0, end, NB) as c0:
                dve.wait_ge(s_win, end * 2 + c0 + 1)
                dve.sem_inc(s_gate)
                with dve.Fori(0, NB) as b:
                    c = c0 + b
                    for s in range(SLOTS):
                        low_one_hot(c, s)
                        w = weigh(c, b, s + 1)
                        add_sums(c, w, s)
                next_round()
            end_pass(p2, 2)

            n2 = [0]

            def link2(ins):
                n2[0] += 1
                ins.then_inc(s_v2, 1)
                dve.wait_ge(s_v2, n2[0])

            def residual2(b):
                v, q = dy_blk(b), b % STATS
                if b >= STATS:
                    dve.wait_ge(s_zd, b - STATS + 1)
                dve.wait_ge(s_c2, b + 1)
                dve.wait_ge(s_yb, b + 1)
                for t in range(BT):
                    o, n = (b % 4) * 1024 + t * P, b * BT + t
                    last = nc.vector.scalar_tensor_tensor(v[:, t, :], ps_flat[:, o:o + P], degn[:, n:n + 1],
                                                          y_all[:, n * P:(n + 1) * P], ALU.mult, ALU.add)
                link2(last)
                normal_statistics(v, q, link2)

            residual2(0)
            for b in range(NBLK):
                if b + 1 < NBLK:
                    residual2(b + 1)
                minus_means(b, 2 * NBLK + b + 1, s_nm)
            assert n2[0] == CHAIN2 * NBLK


_INS = ['x', 'src', 'dst', 'L0_gnn_W1', 'L0_gnn_b1', 'L0_gnn_W2', 'L1_gnn_mlp_w1', 'L1_gnn_mlp_b1',
        'L1_gnn_mlp_w2', 'L1_gnn_mlp_b2', 'L1_gnn_conv_w', 'L1_gnn_conv_b']


def kernel(**inputs):
    import numpy as _np
    import concourse.bacc as _bacc
    from concourse import mybir as _mybir
    from concourse.bass_utils import run_bass_kernel_spmd as _run

    nc = _bacc.Bacc("TRN2", target_bir_lowering=False, num_devices=1)
    arrays, args = {}, []
    for name in _INS:
        a = _np.ascontiguousarray(inputs[name])
        arrays[f"in_{name}_dram"] = a
        args.append(nc.dram_tensor(f"in_{name}_dram", a.shape, _mybir.dt.from_np(a.dtype), kind="ExternalInput").ap())
    shape = inputs["x"].shape
    args.append(nc.dram_tensor("out_0_dram", shape, _mybir.dt.float32, kind="ExternalOutput").ap())
    graph_kernel(nc, *args)
    r = _run(nc, [arrays], core_ids=[0])
    return r.results[0]["out_0_dram"]
```
